# Optimizing a Trainium2 kernel written in Bass

```python
import numpy as np
import jax
import jax.numpy as jnp

def _softmax(x, axis=-1):
    return jax.nn.softmax(x, axis=axis)

def _gelu(x):
    return jax.nn.gelu(x, approximate=True)

def _silu(x):
    return jax.nn.silu(x)

def _sigmoid(x):
    return jax.nn.sigmoid(x)

def _layernorm(x, axis=-1, eps=1e-05):
    m = jnp.mean(x, axis=axis, keepdims=True)
    v = jnp.var(x, axis=axis, keepdims=True)
    return (x - m) / jnp.sqrt(v + eps)

def _scatter_add(tgt, idx, src, axis=0):
    return tgt.at[idx].add(src)

def _segment_sum(src, seg, n):
    return jax.ops.segment_sum(src, seg, n)
kernel_name = 'mk_conv_preact_d2_conv_nhwc512_r2_d96499'

def setup_inputs(seed: int=0):
    np.random.seed(seed)
    _w = jnp.asarray

    def _rec_inputs():
        import jax
        import jax.numpy as jnp
        _gk = jax.random.key(seed)
        x = 1.648e-05 + 1 * jax.random.normal(jax.random.fold_in(_gk, 1), (8, 48, 48, 256), jnp.float32)
        return x
    x = _rec_inputs()

    def _L0_conv_setup():
        import jax, jax.numpy as jnp
        import numpy as np
        D_MODEL = 256
        D_STATE = 16
        EXPAND = 2
        DT_RANK = 8
        D_INNER = EXPAND * D_MODEL
        LN_EPS = 1e-05

        def _ss2d(x, W_in, conv_k, W_xproj, W_dt, b_dt, A_log, Dskip, W_dtN, b_dtN, ln_g, ln_b, W_out, b_out):
            B, H, W_, _ = x.shape
            L = H * W_
            xz = x @ W_in
            xh, z = jnp.split(xz, 2, axis=-1)
            xc = jax.lax.conv_general_dilated(xh, conv_k, window_strides=(1, 1), padding='SAME', dimension_numbers=('NHWC', 'HWIO', 'NHWC'), feature_group_count=D_INNER)
            xp = xc @ W_xproj
            dt_r = xp[..., :DT_RANK]
            Bp = xp[..., DT_RANK:DT_RANK + D_STATE]
            Cp = xp[..., DT_RANK + D_STATE:]
            dt = dt_r @ W_dt + b_dt
            x_seq = xc.reshape(B, L, D_INNER)
            dt_seq = jax.nn.softplus(dt.reshape(B, L, D_INNER))
            B_seq = Bp.reshape(B, L, D_STATE)
            C_seq = Cp.reshape(B, L, D_STATE)
            A = -jnp.exp(A_log)
            dtN = dt_seq @ W_dtN + b_dtN

            def step(h, t):
                x_t, dt_t, dtN_t, B_t, C_t = t
                dA = jnp.exp(dt_t[:, :, None] * A)
                dB = dtN_t * B_t
                h = dA * h + dB[:, None, :] * x_t[:, :, None]
                y = jnp.einsum('bdn,bn->bd', h, C_t) + Dskip * x_t
                return (h, y)
            h0 = jnp.zeros((B, D_INNER, D_STATE), x.dtype)
            xs = (x_seq.transpose(1, 0, 2), dt_seq.transpose(1, 0, 2), dtN.transpose(1, 0, 2), B_seq.transpose(1, 0, 2), C_seq.transpose(1, 0, 2))
            _, ys = jax.lax.scan(step, h0, xs)
            y = ys.transpose(1, 0, 2).reshape(B, H, W_, D_INNER)
            mu = y.mean(-1, keepdims=True)
            var = ((y - mu) ** 2).mean(-1, keepdims=True)
            y = (y - mu) / jnp.sqrt(var + LN_EPS) * ln_g + ln_b
            y = y * jax.nn.silu(z)
            return y @ W_out + b_out
        key = jax.random.key(seed)
        ks = jax.random.split(key, 10)
        B, H, W = (8, 48, 48)
        inp = {'x': jax.random.normal(ks[0], (B, H, W, D_MODEL), jnp.float32), 'W_in': jax.random.normal(ks[1], (D_MODEL, 2 * D_INNER), jnp.float32) * 0.02, 'conv_k': jax.random.normal(ks[2], (3, 3, 1, D_INNER), jnp.float32) * 0.1, 'W_xproj': jax.random.normal(ks[3], (D_INNER, DT_RANK + 2 * D_STATE), jnp.float32) * 0.02, 'W_dt': jax.random.uniform(ks[4], (DT_RANK, D_INNER), jnp.float32, -0.1, 0.1), 'b_dt': jnp.full((D_INNER,), 0.1, jnp.float32), 'A_log': jax.random.normal(ks[5], (D_STATE,), jnp.float32) * 0.02, 'Dskip': jnp.ones((D_INNER,), jnp.float32), 'W_dtN': jax.random.normal(ks[6], (D_INNER, D_STATE), jnp.float32) * 0.02, 'b_dtN': jnp.zeros((D_STATE,), jnp.float32), 'ln_g': jnp.ones((D_INNER,), jnp.float32), 'ln_b': jnp.zeros((D_INNER,), jnp.float32), 'W_out': jax.random.normal(ks[7], (D_INNER, D_MODEL), jnp.float32) * 0.02, 'b_out': jnp.zeros((D_MODEL,), jnp.float32)}
        return inp
    _L0_conv_all = _L0_conv_setup()
    _L0_conv_in = {k: v for k, v in _L0_conv_all.items() if k in ('W_in', 'conv_k', 'W_xproj', 'W_dt', 'b_dt', 'A_log', 'Dskip', 'W_dtN', 'b_dtN', 'ln_g', 'ln_b', 'W_out', 'b_out')}
    del _L0_conv_all

    def _L1_conv_setup():
        import jax, jax.numpy as jnp
        import numpy as np
        TAU = 2.0
        V_THRESHOLD = 1.0
        V_RESET = 0.0
        ATAN_ALPHA = 2.0
        T, B, L, D_IN, D_OUT = (16, 32, 64, 256, 256)

        @jax.custom_vjp
        def atan_spike(x):
            return (x >= 0.0).astype(x.dtype)

        def _atan_spike_fwd(x):
            return (atan_spike(x), x)

        def _atan_spike_bwd(x, g):
            grad = ATAN_ALPHA / 2.0 / (1.0 + (jnp.pi / 2.0 * ATAN_ALPHA * x) ** 2)
            return (g * grad,)
        atan_spike.defvjp(_atan_spike_fwd, _atan_spike_bwd)

        def lif_multistep(h):

            def step(v, x_t):
                v = v + (x_t - (v - V_RESET)) / TAU
                s = atan_spike(v - V_THRESHOLD)
                s_d = jax.lax.stop_gradient(s)
                v = V_RESET * s_d + v * (1.0 - s_d)
                return (v, s)
            v0 = jnp.zeros_like(h[0])
            _, spikes = jax.lax.scan(step, v0, h)
            return spikes
        key = jax.random.key(seed)
        kx, kw, kb = jax.random.split(key, 3)
        x = jax.random.normal(kx, (T, B, L, D_IN), dtype=jnp.float32)
        bound = 1.0 / np.sqrt(D_IN)
        W = jax.random.uniform(kw, (D_OUT, D_IN), minval=-bound, maxval=bound, dtype=jnp.float32)
        b = jax.random.uniform(kb, (D_OUT,), minval=-bound, maxval=bound, dtype=jnp.float32)
        return {'x': x, 'W': W, 'b': b}
    _L1_conv_all = _L1_conv_setup()
    _L1_conv_in = {k: v for k, v in _L1_conv_all.items() if k in ('W', 'b')}
    del _L1_conv_all
    return {'x': x, 'L0_conv_W_in': _L0_conv_in['W_in'], 'L0_conv_conv_k': _L0_conv_in['conv_k'], 'L0_conv_W_xproj': _L0_conv_in['W_xproj'], 'L0_conv_W_dt': _L0_conv_in['W_dt'], 'L0_conv_b_dt': _L0_conv_in['b_dt'], 'L0_conv_A_log': _L0_conv_in['A_log'], 'L0_conv_Dskip': _L0_conv_in['Dskip'], 'L0_conv_W_dtN': _L0_conv_in['W_dtN'], 'L0_conv_b_dtN': _L0_conv_in['b_dtN'], 'L0_conv_ln_g': _L0_conv_in['ln_g'], 'L0_conv_ln_b': _L0_conv_in['ln_b'], 'L0_conv_W_out': _L0_conv_in['W_out'], 'L0_conv_b_out': _L0_conv_in['b_out'], 'L1_conv_W': _L1_conv_in['W'], 'L1_conv_b': _L1_conv_in['b']}

def reference(x, L0_conv_W_in, L0_conv_conv_k, L0_conv_W_xproj, L0_conv_W_dt, L0_conv_b_dt, L0_conv_A_log, L0_conv_Dskip, L0_conv_W_dtN, L0_conv_b_dtN, L0_conv_ln_g, L0_conv_ln_b, L0_conv_W_out, L0_conv_b_out, L1_conv_W, L1_conv_b):
    import jax
    import jax.numpy as jnp

    def _L0_conv_ref(x, W_in, conv_k, W_xproj, W_dt, b_dt, A_log, Dskip, W_dtN, b_dtN, ln_g, ln_b, W_out, b_out):
        import jax, jax.numpy as jnp
        import numpy as np
        D_MODEL = 256
        D_STATE = 16
        EXPAND = 2
        DT_RANK = 8
        D_INNER = EXPAND * D_MODEL
        LN_EPS = 1e-05

        def _ss2d(x, W_in, conv_k, W_xproj, W_dt, b_dt, A_log, Dskip, W_dtN, b_dtN, ln_g, ln_b, W_out, b_out):
            B, H, W_, _ = x.shape
            L = H * W_
            xz = x @ W_in
            xh, z = jnp.split(xz, 2, axis=-1)
            xc = jax.lax.conv_general_dilated(xh, conv_k, window_strides=(1, 1), padding='SAME', dimension_numbers=('NHWC', 'HWIO', 'NHWC'), feature_group_count=D_INNER)
            xp = xc @ W_xproj
            dt_r = xp[..., :DT_RANK]
            Bp = xp[..., DT_RANK:DT_RANK + D_STATE]
            Cp = xp[..., DT_RANK + D_STATE:]
            dt = dt_r @ W_dt + b_dt
            x_seq = xc.reshape(B, L, D_INNER)
            dt_seq = jax.nn.softplus(dt.reshape(B, L, D_INNER))
            B_seq = Bp.reshape(B, L, D_STATE)
            C_seq = Cp.reshape(B, L, D_STATE)
            A = -jnp.exp(A_log)
            dtN = dt_seq @ W_dtN + b_dtN

            def step(h, t):
                x_t, dt_t, dtN_t, B_t, C_t = t
                dA = jnp.exp(dt_t[:, :, None] * A)
                dB = dtN_t * B_t
                h = dA * h + dB[:, None, :] * x_t[:, :, None]
                y = jnp.einsum('bdn,bn->bd', h, C_t) + Dskip * x_t
                return (h, y)
            h0 = jnp.zeros((B, D_INNER, D_STATE), x.dtype)
            xs = (x_seq.transpose(1, 0, 2), dt_seq.transpose(1, 0, 2), dtN.transpose(1, 0, 2), B_seq.transpose(1, 0, 2), C_seq.transpose(1, 0, 2))
            _, ys = jax.lax.scan(step, h0, xs)
            y = ys.transpose(1, 0, 2).reshape(B, H, W_, D_INNER)
            mu = y.mean(-1, keepdims=True)
            var = ((y - mu) ** 2).mean(-1, keepdims=True)
            y = (y - mu) / jnp.sqrt(var + LN_EPS) * ln_g + ln_b
            y = y * jax.nn.silu(z)
            return y @ W_out + b_out
        return _ss2d(x, W_in, conv_k, W_xproj, W_dt, b_dt, A_log, Dskip, W_dtN, b_dtN, ln_g, ln_b, W_out, b_out)

    def _L1_conv_ref(x, W, b):
        import jax, jax.numpy as jnp
        import numpy as np
        TAU = 2.0
        V_THRESHOLD = 1.0
        V_RESET = 0.0
        ATAN_ALPHA = 2.0
        T, B, L, D_IN, D_OUT = (16, 32, 64, 256, 256)

        @jax.custom_vjp
        def atan_spike(x):
            return (x >= 0.0).astype(x.dtype)

        def _atan_spike_fwd(x):
            return (atan_spike(x), x)

        def _atan_spike_bwd(x, g):
            grad = ATAN_ALPHA / 2.0 / (1.0 + (jnp.pi / 2.0 * ATAN_ALPHA * x) ** 2)
            return (g * grad,)
        atan_spike.defvjp(_atan_spike_fwd, _atan_spike_bwd)

        def lif_multistep(h):

            def step(v, x_t):
                v = v + (x_t - (v - V_RESET)) / TAU
                s = atan_spike(v - V_THRESHOLD)
                s_d = jax.lax.stop_gradient(s)
                v = V_RESET * s_d + v * (1.0 - s_d)
                return (v, s)
            v0 = jnp.zeros_like(h[0])
            _, spikes = jax.lax.scan(step, v0, h)
            return spikes
        h = jnp.einsum('tbld,hd->tblh', x, W) + b
        return lif_multistep(h)

    def _gn(v, G=32, eps=1e-05):
        B_, H_, W_, C_ = v.shape
        g = v.reshape(B_, H_, W_, G, C_ // G)
        m = jnp.mean(g, axis=(1, 2, 4), keepdims=True)
        s = jnp.var(g, axis=(1, 2, 4), keepdims=True)
        return ((g - m) / jnp.sqrt(s + eps)).reshape(v.shape)

    def _ln_c(v, eps=1e-06):
        m = jnp.mean(v, axis=-1, keepdims=True)
        s = jnp.var(v, axis=-1, keepdims=True)
        return (v - m) / jnp.sqrt(s + eps)

    def _ln_t(v, eps=1e-05):
        m = jnp.mean(v, axis=-1, keepdims=True)
        s = jnp.var(v, axis=-1, keepdims=True)
        return (v - m) / jnp.sqrt(s + eps)

    def _to_tokens(v):
        B_, H_, W_, C_ = v.shape
        return v.reshape(B_, H_ * W_, C_)

    def _from_tokens(t, like):
        return t.reshape(like.shape)
    x = x + _L0_conv_ref(_gn(x), L0_conv_W_in, L0_conv_conv_k, L0_conv_W_xproj, L0_conv_W_dt, L0_conv_b_dt, L0_conv_A_log, L0_conv_Dskip, L0_conv_W_dtN, L0_conv_b_dtN, L0_conv_ln_g, L0_conv_ln_b, L0_conv_W_out, L0_conv_b_out)
    x = x + _L1_conv_ref(_gn(x), L1_conv_W, L1_conv_b)
    return x

_drawn_inputs = setup_inputs


def setup_inputs(seed=0):
    import zlib

    import numpy as np

    out = dict(_drawn_inputs(seed))
    spreads = {'L0_conv_b_dt': (0.10000000149011612, 0.6),
     'L0_conv_Dskip': (1.0, 0.6),
     'L0_conv_b_dtN': (0.0, 0.8),
     'L0_conv_ln_g': (1.0, 0.6),
     'L0_conv_ln_b': (0.0, 0.8),
     'L0_conv_b_out': (0.0, 0.1)}
    factors = {'L0_conv_W_xproj': 8.0,
     'L0_conv_W_dt': 8.0,
     'L0_conv_A_log': 33.57,
     'L0_conv_W_dtN': 8.0,
     'L1_conv_b': 3.711}
    for name, (base, spread) in spreads.items():
        noise = np.random.default_rng([zlib.crc32(name.encode()), seed]).standard_normal(out[name].shape)
        drawn = base * np.exp(spread * noise) if base else spread * noise
        out[name] = jnp.asarray(drawn.astype(out[name].dtype))
    for name, factor in factors.items():
        out[name] = (out[name] * factor).astype(out[name].dtype)
    return out
```

```python
from contextlib import ExitStack

import concourse.bass as bass
from concourse import mybir

F32 = mybir.dt.float32
BF16 = mybir.dt.bfloat16
ALU = mybir.AluOpType
ACT = mybir.ActivationFunctionType

B, H, W, C = 8, 48, 48, 256
D, NS, RANK = 512, 16, 8
GROUP = 8
P = 128
CH, DC = C // P, D // P
ROWS = 8
T = ROWS * W
K = H // ROWS
NT = T // P
HW = H * W
HALO = (ROWS + 2) * W
WP = W + 2
TAPS = 9
LN_EPS = GN_EPS = 1e-5
EXP_CAP = float(2 ** 60)

PART_ROW = (0, 64, 96)
DT_ROW = 32
XP_ROWS = PART_ROW[2] + NS

NWORK = 4
NHT = 4

PRE, POST, L1, TIN, GN1 = "pre", "post", "l1", "tin", "gn1"
L1_CHUNKS = {1: (0, 1), 2: (2, 3), 3: (4, 5)}
TIN_CHUNKS = {2: (0, 1), 3: (2, 3), 4: (4, 5)}
CONV_PARTS = {2: [(0, 0, 7)], 3: [(0, 7, 9), (1, 0, 5)], 4: [(1, 5, 9), (2, 0, 3)],
              5: [(2, 3, 9), (3, 0, 1)], 6: [(3, 1, 9)]}


def groups(k, s):
    out = []
    if s < 14:
        out.append(("main", f"bb{s + 2}"))
    if s == 0:
        out += [(PRE, "xh0"), (PRE, "xh1")]
    if s == 1:
        out.append((PRE, "xh2"))
    if s == 4:
        out.append((PRE, "xh3"))
    for d, lo, _ in CONV_PARTS.get(s, ()):
        if lo == 0:
            out.append((PRE, f"cv{d}"))
    if s == 7:
        out += [(PRE, "xp"), (PRE, "ct"), (PRE, "dt0"), (PRE, "dt1")]
    if s == 8:
        out += [(PRE, "dt2"), (PRE, "dt3")]
    if s == 9:
        out += [(POST, f"bt{d}") for d in range(DC)]
    if s == 11:
        out.append((PRE, "dn"))
    if s == 12:
        out += [(POST, f"z{d}") for d in range(DC)]
    if s == 14:
        out += [(POST, "wo0"), (POST, "wo1"), (PRE, "bb0")]
    if s == 15:
        out += [(PRE, "bb1"), (PRE, "yi0"), (PRE, "yi1"), (PRE, "yi2")]
    if k in L1_CHUNKS:
        a, b = L1_CHUNKS[k]
        out += {8: [(L1, f"l{a}_0"), (L1, f"l{a}_1")], 10: [(L1, f"to{a}_0"), (L1, f"to{a}_1")],
                11: [(L1, f"l{b}_0"), (L1, f"l{b}_1")], 13: [(L1, f"to{b}_0"), (L1, f"to{b}_1")]}.get(s, [])
    if k in TIN_CHUNKS:
        a, b = TIN_CHUNKS[k]
        out += {6: [(TIN, f"ti{a}_0"), (TIN, f"ti{a}_1")], 12: [(TIN, f"ti{b}_0"), (TIN, f"ti{b}_1")]}.get(s, [])
    if k == 1:
        out += {1: [(GN1, "gm1")], 2: [(GN1, "gv1")], 4: [(GN1, "b1")]}.get(s, [])
    if k == 4:
        out += {14: [(TIN, "gm0")], 15: [(TIN, "gv0")]}.get(s, [])
    return out


def does(b, k):
    if not isinstance(b, int):
        return {"main", PRE, POST, L1, TIN, GN1}
    kinds = set()
    if 0 <= b < B:
        kinds.add("main")
    if 0 <= b * K + k + 1 < B * K:
        kinds.add(PRE)
    if 0 <= b * K + k - 1 < B * K:
        kinds.add(POST)
    if 1 <= b <= B:
        kinds |= {L1, GN1}
    if -1 <= b < B - 1:
        kinds.add(TIN)
    return kinds


def bank_turns():
    turns, fills = {}, [0] * NWORK
    for b in range(-1, B + 1):
        for k in range(K):
            n = 0
            for s in range(NS):
                for kind, name in groups(k, s):
                    if kind in does(b, k):
                        turns[b, k, name] = (n % NWORK, fills[n % NWORK])
                        fills[n % NWORK] += 1
                    n += 1
    return turns


TURNS = bank_turns()


def turn(b, k, name):
    back = 0
    while k < 0:
        k, back = k + K, back + 1
    if isinstance(b, int):
        return TURNS.get((b - back, k, name))
    known = {i: TURNS[i - back, k, name] for i in range(1, B - 1) if (i - back, k, name) in TURNS}
    bank, last = known[B - 2]
    growth = last - known[B - 3][1]
    assert all(known[i] == (bank, last - (B - 2 - i) * growth) for i in known)
    assert last - (B - 3) * growth >= 0
    return bank, b * growth + (last - (B - 2) * growth)


def vssm_lif_kernel(nc, x, w_in, conv_k, w_xproj, w_dt, b_dt, a_log, dskip, w_dtn, b_dtn, ln_g, ln_b,
                    w_out, b_out, w1, b1, out):
    ctx = ExitStack()
    with ctx:
        def sb(name, shape, dt=F32):
            return ctx.enter_context(nc.sbuf_tensor(name, shape, dt))

        def sem(name):
            return ctx.enter_context(nc.semaphore(name))

        ident = sb("ident", [P, P])
        group_mean = sb("group_mean", [P, P])
        win = sb("win", [P, CH, 2 * D])
        taps = sb("taps", [P, DC, TAPS])
        conv_diag = sb("conv_diag", [P, DC, TAPS, P])
        skip_diag = sb("skip_diag", [P, DC, P])
        skip = sb("skip", [P, DC])
        wx = sb("wx", [P, DC, RANK + 2 * NS])
        wxp = sb("wxp", [P, DC, XP_ROWS])
        wn = sb("wn", [P, DC, NS])
        wnp = sb("wnp", [P, DC, XP_ROWS])
        bn_rows = sb("bn_rows", [XP_ROWS, 1])
        wdt = sb("wdt", [XP_ROWS, D])
        bdt = sb("bdt", [P, DC])
        neg_a = sb("neg_a", [P, NS])
        a_raw = sb("a_raw", [P, NS])
        gamma = sb("gamma", [P, DC])
        beta = sb("beta", [P, DC])
        wo = sb("wo", [P, DC, C])
        bo = sb("bo", [P, CH])
        w1t = sb("w1t", [P, CH, C])
        w1s = sb("w1s", [P, CH, C])
        b1c = sb("b1c", [P, CH])
        b1s = sb("b1s", [P, CH])
        one_hot = sb("one_hot", [XP_ROWS, NS], BF16)
        half_neg = sb("half_neg", [P, 4])

        img = sb("img", [P, 2, CH, HW])
        volt = sb("volt", [P, CH, HW])
        xin = sb("xin", [P, NT, C])
        xn = sb("xn", [P, 3, CH, HALO])
        xhp = sb("xhp", [P, 3, ROWS + 2, WP])
        xc = sb("xc", [P, 2, DC, T])
        dt = sb("dt", [P, 2, DC, T])
        xb = sb("xb", [P, DC, T])
        xp = sb("xp", [XP_ROWS, T])
        ct = sb("ct", [P, 2, NT * NS])
        bprod = sb("bprod", [XP_ROWS, T])
        bparts = sb("bparts", [XP_ROWS, 2, T], BF16)
        bbc = sb("bbc", [P, 3, T])
        decay = sb("decay", [P, 2, DC, T])
        st = sb("st", [P, 3, DC, T])
        carry = sb("carry", [P, DC, NS])
        y = sb("y", [P, 2, NT, D])
        zs = xb
        ob = sb("ob", [P, CH, T])
        ot = sb("ot", [P, NT, C])
        ln_st = sb("ln_st", [P, NT, 6])
        ln_mv = sb("ln_mv", [P, NT, 2])
        ln_ve = sb("ln_ve", [P, NT])
        ln_rs = sb("ln_rs", [P, NT])
        ln_mr = sb("ln_mr", [P, NT])
        ln_nb = sb("ln_nb", [P, NT])
        gn_st = [sb(f"gn_st{w}", [P, CH, K * 6]) for w in range(2)]
        gn_mv = [sb(f"gn_mv{w}", [P, CH, 2]) for w in range(2)]
        gn_mu = [sb(f"gn_mu{w}", [P, CH]) for w in range(2)]
        gn_dm = [sb(f"gn_dm{w}", [P, CH]) for w in range(2)]
        gn_sq = [sb(f"gn_sq{w}", [P, CH]) for w in range(2)]
        gn_dv = [sb(f"gn_dv{w}", [P, CH]) for w in range(2)]
        gn_ve = [sb(f"gn_ve{w}", [P, CH]) for w in range(2)]
        gn_rs = [sb(f"gn_rs{w}", [P, CH]) for w in range(2)]
        gn_mr = [sb(f"gn_mr{w}", [P, CH]) for w in range(2)]
        gn_nb = [sb(f"gn_nb{w}", [P, CH]) for w in range(2)]

        work = ctx.enter_context(nc.psum_tensor("work", [P, NWORK, 512], F32))
        ht = ctx.enter_context(nc.psum_tensor("ht", [P, NHT, 512], F32))

        s_w = sem("weights_loaded")
        s_w1 = sem("w1_loaded")
        s_set_pool = sem("constants_by_pool")
        s_set_dve = sem("constants_by_dve")
        s_set_act = sem("constants_by_act")
        s_setp = sem("w1_transposed")
        filled = [sem(f"work_bank{i}_filled") for i in range(NWORK)]
        emptied = [sem(f"work_bank{i}_emptied") for i in range(NWORK)]
        s_xin = sem("x_tile_loaded")
        s_gst = [sem(f"gn{w}_stats") for w in range(2)]
        s_gag = [sem(f"gn{w}_channel_means") for w in range(2)]
        s_gdv = [sem(f"gn{w}_by_dve") for w in range(2)]
        s_gpl = [sem(f"gn{w}_scale_and_shift") for w in range(2)]
        s_xn = sem("xn_ready")
        s_exp = sem("dt_exp")
        s_cap = sem("dt_capped")
        s_ln = sem("dt_log")
        s_dt = sem("dt_ready")
        s_split = sem("b_split")
        s_dec = sem("decay_ready")
        s_u = sem("scan_input_ready")
        s_scan = sem("scans_done")
        s_ht = sem("states_transposed")
        s_y = sem("y_accumulated")
        s_carry = sem("carry_saved")
        s_lnst = sem("ln_stats")
        s_lnmv = sem("ln_mean_var")
        s_lnve = sem("ln_var_eps")
        s_lnp = sem("ln_by_pool")
        s_yz = sem("y_gated")
        s_w1s = sem("w1_scaled")
        s_lif = sem("lif_steps")
        s_out = sem("out_tile_stored")
        s_edge = sem("xn_edge_zeroed")
        s_hold = {e: sem(f"{e}_wait_held") for e in ("pool", "act", "dve")}

        block = ctx.enter_context(nc.Block())

        def need(eng, s, value):
            if not isinstance(value, int) or value > 0:
                eng.wait_ge(s, value)

        def hold(name, eng, b):
            if not isinstance(b, int):
                eng.sem_inc(s_hold[name], 1)

        def await_filled(eng, b, k, name):
            at = turn(b, k, name)
            if at is not None:
                eng.wait_ge(filled[at[0]], at[1] + 1)
                return at[0]

        def await_emptied(eng, b, k, name):
            at = turn(b, k, name)
            if at is not None:
                eng.wait_ge(emptied[at[0]], at[1] + 1)

        def claim(pe, b, k, name):
            i, before = turn(b, k, name)
            need(pe, emptied[i], before)
            return i

        def img_par(b, d=0):
            return (b + d + 2) % 2

        def walk(eng, iteration):
            for k in range(2, K):
                iteration(-1, k)
            for k in range(K):
                iteration(0, k)
            with eng.Fori(1, B - 1, 1) as b:
                for k in range(K):
                    iteration(b, k)
            for k in range(K):
                iteration(B - 1, k)
            for k in range(4):
                iteration(B, k)

        x_v = x.rearrange("b (k r) w c -> b k (r w) c", r=ROWS)
        out_v = out.rearrange("b (k r) w c -> b k (r w) c", r=ROWS)

        @block.sync
        def _(sp):
            def load(dst, src):
                sp.dma_start(dst, src, allow_slow_non_contiguous=True).then_inc(s_w, 16)

            def load_x(b, kc, d):
                before = {0: 4 - K, 1: 2, 2: 2, 3: 3, 4: 3, 5: 4}[kc]
                await_filled(sp, b, before, f"ti{(kc - 1) % K}_1")
                sp.dma_start(xin[:, :, :], x_v[b + d, kc].rearrange("(m p) c -> p m c", p=P)).then_inc(s_xin, 16)

            sp.sem_inc(s_out, 16)
            load_x(-1, 0, 1)
            load(win[:, :, :], w_in.rearrange("(h p) n -> p h n", p=P))
            for c in range(DC):
                sp.dma_start(taps[:, c, :], conv_k.rearrange("i j o d -> d (i j o)")[c * P:(c + 1) * P, :],
                             allow_slow_non_contiguous=True).then_inc(s_w, 16)
            load(wx[:, :, :], w_xproj.rearrange("(c p) n -> p c n", p=P))
            load(wn[:, :, :], w_dtn.rearrange("(c p) n -> p c n", p=P))
            load(wo[:, :, :], w_out.rearrange("(c p) n -> p c n", p=P))
            for v, t in ((b_dt, bdt), (dskip, skip), (ln_g, gamma), (ln_b, beta), (b_out, bo), (b1, b1c)):
                load(t[:, :], v.rearrange("(c p) -> p c", p=P))
            load(a_raw[:, :], a_log.rearrange("(o n) -> o n", o=1).to_broadcast([P, NS]))
            sp.dma_start(w1s[:, :, :], w1.rearrange("(h p) n -> p h n", p=P)).then_inc(s_w1, 16)
            sp.wait_ge(s_set_pool, 1)
            load(wdt[DT_ROW:DT_ROW + RANK, :], w_dt)
            for r in PART_ROW:
                load(bn_rows[r:r + NS, :], b_dtn.rearrange("(n o) -> n o", o=1))

            def store(b, kc):
                await_emptied(sp, b, {0: 1, 1: 1, 2: 2, 3: 2, 4: 3, 5: 3}[kc], f"to{kc}_1")
                sp.dma_start(out_v[b - 1, kc].rearrange("(m p) c -> p m c", p=P),
                             ot[:, :, :]).then_inc(s_out, 16)

            def iteration(b, k):
                do = does(b, k)
                tin = TIN_CHUNKS.get(k, ()) if TIN in do else ()
                l1 = L1_CHUNKS.get(k, ()) if L1 in do else ()
                for n in range(2):
                    if tin and not (isinstance(b, int) and b == -1 and tin[n] == 0):
                        load_x(b, tin[n], 1)
                    if l1:
                        store(b, l1[n])

            walk(sp, iteration)
            sp.wait_ge(s_out, B * K * 16 + 16)

        N_W = (1 + DC + 3 + 6 + 1 + 1 + 3) * 16

        @block.gpsimd
        def _(pool):
            g = nc.gpsimd
            g.memset(wdt[:, :], 0.0)
            g.memset(wxp[:, :, :], 0.0)
            g.memset(wnp[:, :, :], 0.0)
            g.memset(one_hot[:, :], 0.0)
            g.memset(half_neg[:, :], -0.5)
            g.memset(xhp[:, :, :, :], 0.0)
            g.memset(volt[:, :, :], 0.0)
            g.memset(ident[:, :], 0.0)
            g.memset(group_mean[:, :], 1.0 / GROUP)
            g.memset(bn_rows[:, :], 0.0).then_inc(s_set_pool, 1)
            pool.wait_ge(s_set_pool, 1)
            g.affine_select(out=ident[:, :], in_=ident[:, :], compare_op=ALU.not_equal, fill=1.0, base=0,
                            pattern=[[-1, P]], channel_multiplier=1)
            gm = group_mean[:, :].rearrange("p (g e) -> p g e", e=GROUP)
            g.affine_select(out=gm, in_=gm, compare_op=ALU.is_ge, fill=0.0, base=0,
                            pattern=[[-GROUP, P // GROUP], [0, GROUP]],
                            channel_multiplier=1).then_inc(s_set_pool, 1)
            pool.wait_ge(s_set_pool, 2)
            g.affine_select(out=gm, in_=gm, compare_op=ALU.is_ge, fill=0.0, base=GROUP - 1,
                            pattern=[[GROUP, P // GROUP], [0, GROUP]],
                            channel_multiplier=-1).then_inc(s_set_pool, 1)
            pool.wait_ge(s_w, N_W)
            pool.wait_ge(s_set_pool, 3)
            for c in range(DC):
                g.tensor_scalar(skip_diag[:, c, :], ident[:, :], skip[:, c:c + 1], None, ALU.mult)
                for t in range(TAPS):
                    last = g.tensor_scalar(conv_diag[:, c, t, :], ident[:, :], taps[:, c, t:t + 1], None, ALU.mult)
            last.then_inc(s_set_pool, 1)

            def scale_input(w, e, b, k):
                await_emptied(pool, b, k, f"gv{w}")
                g.tensor_tensor(gn_rs[w][:, :], gn_ve[w][:, :], half_neg[:, 0:CH], ALU.pow).then_inc(s_gpl[w], 1)
                pool.wait_ge(s_gpl[w], e * 3 + 1)
                g.tensor_tensor(gn_mr[w][:, :], gn_mu[w][:, :], gn_rs[w][:, :], ALU.mult).then_inc(s_gpl[w], 1)
                pool.wait_ge(s_gpl[w], e * 3 + 2)
                hold("pool", pool, b)
                g.tensor_scalar(gn_nb[w][:, :], gn_mr[w][:, :], -1.0, 0.0, ALU.mult, ALU.add).then_inc(s_gpl[w], 1)

            def zero_edges(b, k):
                k1 = (k + 1) % K
                if k1 in (0, K - 1):
                    await_filled(pool, b, k - 1, f"z{DC - 1}")
                    hold("pool", pool, b)
                    edge = slice(0, W) if k1 == 0 else slice(HALO - W, HALO)
                    g.memset(xn[:, k1 % 3, :, edge], 0.0).then_inc(s_edge, 1)

            def scan_input(b, k, n, ahead):
                kq = (k + ahead) % K
                i = (b * K + k + ahead) * NS + n
                j = (kq * NS + n) % 3
                await_emptied(pool, b, k - 1 if n == 1 else k, f"bb{n}")
                need(pool, s_y, 3 * (i - 2))
                if n == 0:
                    await_emptied(pool, b, k, f"cv{DC - 1}")
                g.tensor_tensor(st[:, j, :, :], xc[:, kq % 2, :, :],
                                bbc[:, j, :].unsqueeze(1).to_broadcast([P, DC, T]),
                                ALU.mult).then_inc(s_u, 1)

            def split(b, k):
                q1 = b * K + k + 1
                kq = (k + 1) % K
                par = kq % 2
                await_emptied(pool, b, k, "dn")
                await_filled(pool, b, k - 1, f"bb{NS - 1}")
                _, r2, r3 = PART_ROW
                hold("pool", pool, b)
                g.tensor_copy(bparts[:, par, :], bprod[:, :]).then_inc(s_split, 1)
                pool.wait_ge(s_split, q1 * 5 + 1)
                g.tensor_tensor(bprod[r2:XP_ROWS, :], bprod[r2:XP_ROWS, :], bparts[r2:XP_ROWS, par, :],
                                ALU.subtract).then_inc(s_split, 1)
                pool.wait_ge(s_split, q1 * 5 + 2)
                hold("pool", pool, b)
                g.tensor_copy(bparts[r2:XP_ROWS, par, :], bprod[r2:XP_ROWS, :]).then_inc(s_split, 1)
                pool.wait_ge(s_split, q1 * 5 + 3)
                g.tensor_tensor(bprod[r3:XP_ROWS, :], bprod[r3:XP_ROWS, :], bparts[r3:XP_ROWS, par, :],
                                ALU.subtract).then_inc(s_split, 1)
                pool.wait_ge(s_split, q1 * 5 + 4)
                hold("pool", pool, b)
                g.tensor_copy(bparts[r3:XP_ROWS, par, :], bprod[r3:XP_ROWS, :]).then_inc(s_split, 1)
                pool.wait_ge(s_split, q1 * 5 + 5)

            def iteration(b, k):
                do = does(b, k)
                q0 = b * K + k - 1
                p0 = (k - 1) % 2
                for s in range(NS):
                    if s == 0 and PRE in do:
                        zero_edges(b, k)
                    if s < NS - 1 and "main" in do:
                        scan_input(b, k, s + 1, 0)
                    if s == NS - 1 and PRE in do:
                        scan_input(b, k, 0, 1)
                    if s == 1 and POST in do:
                        pool.wait_ge(s_lnve, q0 + 1)
                        g.tensor_tensor(ln_rs[:, :], ln_ve[:, :], half_neg[:, 0:NT], ALU.pow).then_inc(s_lnp, 1)
                        pool.wait_ge(s_lnp, q0 * 6 + 1)
                        g.tensor_tensor(ln_mr[:, :], ln_mv[:, :, 0], ln_rs[:, :], ALU.mult).then_inc(s_lnp, 1)
                        pool.wait_ge(s_lnp, q0 * 6 + 2)
                        hold("pool", pool, b)
                        g.tensor_scalar(ln_nb[:, :], ln_mr[:, :], -1.0, 0.0, ALU.mult, ALU.add).then_inc(s_lnp, 1)
                    if s == 2 and POST in do:
                        pool.wait_ge(s_lnp, q0 * 6 + 3)
                        hold("pool", pool, b)
                        for m in range(NT):
                            g.tensor_scalar(y[:, p0, m, :], y[:, p0, m, :], ln_rs[:, m:m + 1], ln_nb[:, m:m + 1],
                                            ALU.mult, ALU.add).then_inc(s_lnp, 1)
                    if s == 9 and PRE in do:
                        pool.wait_ge(s_exp, b * K + k + 2)
                        dn = dt[:, (k + 1) % 2, :, :]
                        hold("pool", pool, b)
                        g.tensor_scalar(dn, dn, EXP_CAP, 0.0, ALU.min, ALU.max).then_inc(s_cap, 1)
                    if s == 13 and POST in do:
                        yg = y[:, p0, :, :].rearrange("p m d -> p (m d)").rearrange("p (c t) -> p c t", c=DC)
                        for c in range(DC):
                            await_emptied(pool, b, k, f"z{c}")
                            await_emptied(pool, b, k, f"bt{c}")
                            g.tensor_tensor(zs[:, c, :], zs[:, c, :], yg[:, c, :], ALU.mult).then_inc(s_yz, 1)
                    if s == 12 and PRE in do:
                        split(b, k)
                    if s == 15 and k == 4 and TIN in do:
                        scale_input(0, b + 1, b, k)
                    if s == 3 and k == 1 and GN1 in do:
                        await_filled(pool, b, 1 - K, "b1")
                        pool.wait_ge(s_setp, 1)
                        await_filled(pool, b, 3 - K, "l5_1")
                        scale_input(1, b - 1, b, k)
                        pool.wait_ge(s_gpl[1], (b - 1) * 3 + 3)
                        hold("pool", pool, b)
                        for h in range(CH):
                            last = g.tensor_scalar(w1s[:, h, :], w1t[:, h, :], gn_rs[1][:, h:h + 1], 0.0,
                                                   ALU.mult, ALU.add)
                        last.then_inc(s_w1s, 1)

            walk(pool, iteration)

        @block.scalar
        def _(act):
            a = nc.scalar
            TABLES = "natural_log_exp_and_others"
            a.preload_act_table_set(TABLES)
            act.wait_ge(s_w, N_W)
            a.activation(neg_a[:, :], a_raw[:, :], ACT.Exp).then_inc(s_set_act, 1)

            def iteration(b, k):
                do = does(b, k)
                q0, q1 = b * K + k - 1, b * K + k + 1
                k1 = (k + 1) % K
                p0, p1 = (k - 1) % 2, k1 % 2
                main, pre, post = "main" in do, PRE in do, POST in do

                def bank_copy(name, dst, cols, rows=P, view=lambda v: v, func=ACT.Copy, **kw):
                    i = await_filled(act, b, k, name)
                    if name[:2] == "ti":
                        hold("act", act, b)
                    a.activation(dst, view(work[0:rows, i, 0:cols]), func, **kw).then_inc(emptied[i], 1)

                for s in range(NS):
                    if s == 0 and pre:
                        d = 1 if k == K - 1 else 0
                        act.wait_ge(s_gpl[0], (b + d) * 3 + 3)
                        await_filled(act, b, k - 1, f"z{DC - 1}")
                        hold("act", act, b)
                        lo = k1 * T - W
                        r0, r1 = (W if k1 == 0 else 0), (HALO - W if k1 == K - 1 else HALO)
                        for h in range(CH):
                            last = a.activation(xn[:, k1 % 3, h, r0:r1], img[:, img_par(b, d), h, lo + r0:lo + r1],
                                                ACT.Identity, bias=gn_nb[0][:, h:h + 1], scale=gn_rs[0][:, h:h + 1])
                        last.then_inc(s_xn, 1)
                    if s == 9 and pre:
                        await_emptied(act, b, k, f"dt{DC - 1}")
                        a.activation(dt[:, p1, :, :], xb[:, :, :], ACT.Exp).then_inc(s_exp, 1)
                    if s == 10 and pre:
                        act.wait_ge(s_cap, q1 + 1)
                        a.activation(dt[:, p1, :, :], dt[:, p1, :, :], ACT.Ln, bias=1.0).then_inc(s_ln, 1)
                    for c, _, hi in CONV_PARTS.get(s, ()):
                        if hi == TAPS and pre:
                            if c == 0:
                                need(act, s_u, (q1 - 1) * NS)
                            bank_copy(f"cv{c}", xc[:, p1, c, :], T)
                    silu = False
                    for kind, name in groups(k, s):
                        if kind not in do:
                            continue
                        if name[:2] == "bb":
                            n = int(name[2:])
                            i = (q1 if n < 2 else q1 - 1) * NS + n
                            need(act, s_u, i - 2)
                            kq = k1 if n < 2 else k
                            bank_copy(name, bbc[:, (kq * NS + n) % 3, :], T)
                        elif name[:2] == "xh":
                            c = int(name[2:])
                            if c == 0:
                                await_filled(act, b, k - 1, "cv3")
                            if c == 1:
                                await_filled(act, b, k - 1, "cv1")
                            if c == 2:
                                await_filled(act, b, k - 1, "cv2")
                            if c == 3:
                                await_filled(act, b, k, "cv0")
                            bank_copy(name, xhp[:, c % 3, :, 1:1 + W], HALO,
                                          view=lambda v: v.rearrange("p (r w) -> p r w", w=W))
                        elif name[:2] == "cv":
                            continue
                        elif name == "xp":
                            await_emptied(act, b, k - 1, "dn")
                            bank_copy(name, xp[:, :], T, XP_ROWS)
                        elif name == "ct":
                            need(act, s_y, (q1 - 1) * NS * NT)
                            bank_copy(name, ct[:, p1, :], NT * NS)
                        elif name[:2] == "dt":
                            c = int(name[2:])
                            if c == 0:
                                await_filled(act, b, k - 1, "wo1")
                            bank_copy(name, xb[:, c, :], T, func=ACT.Identity, bias=bdt[:, c:c + 1])
                        elif name[:2] == "bt":
                            c = int(name[2:])
                            yg = y[:, p0, :, :].rearrange("p m d -> p (m d)").rearrange("p (c t) -> p c t", c=DC)
                            await_filled(act, b, k, f"bt{DC - 1}")
                            bank_copy(name, yg[:, c, :], T, func=ACT.Identity,
                                          bias=beta[:, c:c + 1], scale=gamma[:, c:c + 1])
                        elif name[0] == "z":
                            c = int(name[1:])
                            if c == 0:
                                if pre:
                                    act.wait_ge(s_dt, q1 + 1)
                                else:
                                    await_filled(act, b, k - 1, "wo1")
                            bank_copy(name, zs[:, c, :], T, func=ACT.Silu)
                            silu = True
                        elif name[:2] == "yi":
                            m = int(name[2:])
                            need(act, s_yz, (q1 - 1) * DC)
                            bank_copy(name, y[:, p1, m, :], D)
                        elif name[:2] == "ti":
                            kc, h = int(name[2]), int(name[4])
                            if not (isinstance(b, int) and b < 1):
                                act.wait_ge(s_lif, ((b - 1) * K + kc) * 6 + 6)
                            bank_copy(name, img[:, img_par(b, 1), h, kc * T:(kc + 1) * T], T)
                        elif name[:2] == "to":
                            kc, half = int(name[2]), int(name[4])
                            if half == 0:
                                act.wait_ge(s_out, ((b - 1) * K + kc) * 16 + 16)
                            dst = ot[:, 0:2, :] if half == 0 else ot[:, 2:3, :]
                            n = 2 if half == 0 else 1
                            bank_copy(name, dst, n * C, view=lambda v, n=n: v.rearrange("p (m c) -> p m c", m=n))
                    if silu:
                        a.preload_act_table_set(TABLES)
                    n = (s + 1) % NS
                    if (main if s < NS - 1 else pre):
                        ahead = 1 if s == NS - 1 else 0
                        qn = b * K + k + ahead
                        i = qn * NS + n
                        need(act, s_scan, i - 1)
                        if n == 0:
                            act.wait_ge(s_dt, qn + 1)
                            if isinstance(b, int) and b == -1:
                                act.wait_ge(s_set_dve, 3)
                        a.activation(decay[:, n % 2, :, :], dt[:, (k + ahead) % 2, :, :], ACT.Exp,
                                     scale=neg_a[:, n:n + 1]).then_inc(s_dec, 1)

            walk(act, iteration)

        @block.vector
        def _(dve):
            v = nc.vector
            dve.wait_ge(s_w, N_W)
            dve.wait_ge(s_set_pool, 3)
            r1, r2, r3 = PART_ROW
            for r in PART_ROW:
                v.tensor_copy(wxp[:, :, r:r + NS], wx[:, :, RANK:RANK + NS])
                v.tensor_copy(wnp[:, :, r:r + NS], wn[:, :, :])
                v.tensor_copy(one_hot[r:r + NS, :], ident[r:r + NS, r:r + NS])
            v.tensor_copy(wxp[:, :, DT_ROW:DT_ROW + RANK], wx[:, :, 0:RANK]).then_inc(s_set_dve, 1)
            dve.wait_ge(s_setp, 1)
            v.tensor_copy(w1t[:, :, :].rearrange("p h n -> p (h n)"), ht[:, 0, :]).then_inc(s_set_dve, 1)
            dve.wait_ge(s_set_act, 1)
            dve.wait_ge(s_set_dve, 2)
            v.tensor_scalar(neg_a[:, :], neg_a[:, :], -1.0, None, ALU.mult).then_inc(s_set_dve, 1)

            def channel_means(w, e):
                dve.wait_ge(s_gst[w], (e + 1) * CH * K)
                hold("dve", dve, e)
                for h in range(CH):
                    v.bn_aggr(gn_mv[w][:, h, :], gn_st[w][:, h, :]).then_inc(s_gag[w], 1)

            def group_deviation(w, e, b, k):
                i = await_filled(dve, b, k, f"gm{w}")
                v.tensor_copy(gn_mu[w][:, :], work[:, i, 0:CH]).then_inc(emptied[i], 1)
                await_emptied(dve, b, k, f"gm{w}")
                v.tensor_tensor(gn_dm[w][:, :], gn_mv[w][:, :, 0], gn_mu[w][:, :], ALU.subtract).then_inc(s_gdv[w], 1)
                dve.wait_ge(s_gdv[w], e * 3 + 1)
                v.tensor_tensor(gn_sq[w][:, :], gn_dm[w][:, :], gn_dm[w][:, :], ALU.mult).then_inc(s_gdv[w], 1)
                dve.wait_ge(s_gdv[w], e * 3 + 2)
                v.tensor_tensor(gn_dv[w][:, :], gn_sq[w][:, :], gn_mv[w][:, :, 1], ALU.add).then_inc(s_gdv[w], 1)

            def group_variance(w, b, k):
                i = await_filled(dve, b, k, f"gv{w}")
                v.tensor_scalar(gn_ve[w][:, :], work[:, i, 0:CH], GN_EPS, None, ALU.add).then_inc(emptied[i], 1)

            def lif(b, k, kc):
                il = (b - 1) * K + kc
                par = img_par(b, -1)
                cols = slice(kc * T, (kc + 1) * T)
                if kc == 0:
                    await_emptied(dve, b, 1, "b1")
                await_filled(dve, b, {0: 3 - K, 1: 1, 2: 1, 3: 2, 4: 2, 5: 3}[kc], f"to{(kc - 1) % K}_1")
                for h in range(CH):
                    i = await_filled(dve, b, k, f"l{kc}_{h}")
                    v.scalar_tensor_tensor(out=ob[:, h, :], in0=work[:, i, 0:T], scalar=b1s[:, h:h + 1],
                                           in1=volt[:, h, cols], op0=ALU.add, op1=ALU.subtract).then_inc(emptied[i], 1)
                for h in range(CH):
                    await_emptied(dve, b, k, f"l{kc}_{h}")
                    v.scalar_tensor_tensor(out=volt[:, h, cols], in0=ob[:, h, :], scalar=0.5,
                                           in1=volt[:, h, cols], op0=ALU.mult, op1=ALU.add).then_inc(s_lif, 1)
                for h in range(CH):
                    dve.wait_ge(s_lif, il * 6 + 1 + h)
                    v.scalar_tensor_tensor(out=ob[:, h, :], in0=volt[:, h, cols], scalar=1.0,
                                           in1=img[:, par, h, cols], op0=ALU.is_ge, op1=ALU.add).then_inc(s_lif, 1)
                for h in range(CH):
                    v.scalar_tensor_tensor(out=volt[:, h, cols], in0=volt[:, h, cols], scalar=1.0,
                                           in1=volt[:, h, cols], op0=ALU.is_lt, op1=ALU.mult).then_inc(s_lif, 1)

            def accumulate(b, k, n, before):
                kq = (k - before) % K
                q = b * K + k - before
                i = q * NS + n
                for m in range(NT):
                    dve.wait_ge(s_ht, 3 * i + m + 1)
                    if n == 0:
                        if m == 0:
                            await_emptied(dve, b, k - 1, "ct")
                        await_emptied(dve, b, k - 1, f"yi{m}")
                    else:
                        dve.wait_ge(s_y, 3 * (i - 1) + m + 1)
                    j = (3 * n + m) % NHT
                    v.scalar_tensor_tensor(out=y[:, kq % 2, m, :], in0=ht[:, j, :],
                                           scalar=ct[:, kq % 2, m * NS + n:m * NS + n + 1],
                                           in1=y[:, kq % 2, m, :], op0=ALU.mult, op1=ALU.add).then_inc(s_y, 1)

            def iteration(b, k):
                do = does(b, k)
                q0, q1 = b * K + k - 1, b * K + k + 1
                k1 = (k + 1) % K
                p0, p1 = (k - 1) % 2, k1 % 2
                main, pre, post = "main" in do, PRE in do, POST in do
                for s in range(NS):
                    i = (b * K + k) * NS + s
                    j = (k * NS + s) % 3
                    if main:
                        dve.wait_ge(s_dec, i + 1)
                        dve.wait_ge(s_u, i + 1)
                        if k > 0:
                            dve.wait_ge(s_carry, (b * (K - 1) + k - 1) * NS + s + 1)
                        for c in range(DC):
                            first = 0.0 if k == 0 else carry[:, c, s:s + 1]
                            last = v.tensor_tensor_scan(st[:, j, c, :], decay[:, s % 2, c, :], st[:, j, c, :],
                                                        first, ALU.mult, ALU.add)
                        last.then_inc(s_scan, 1)
                    if s > 0 and main:
                        accumulate(b, k, s - 1, 0)
                    if s == 0 and post:
                        accumulate(b, k, NS - 1, 1)
                    if main and k < K - 1:
                        dve.wait_ge(s_scan, i + 1)
                        v.tensor_copy(carry[:, :, s], st[:, j, :, T - 1]).then_inc(s_carry, 1)
                    if s == 0 and post:
                        for m in range(NT):
                            dve.wait_ge(s_y, (q0 * NS + NS - 1) * 3 + m + 1)
                            v.bn_stats(ln_st[:, m, :], y[:, p0, m, :]).then_inc(s_lnst, 1)
                        for m in range(NT):
                            dve.wait_ge(s_lnst, q0 * NT + m + 1)
                            hold("dve", dve, b)
                            v.bn_aggr(ln_mv[:, m, :], ln_st[:, m, :]).then_inc(s_lnmv, 1)
                        dve.wait_ge(s_lnmv, q0 * NT + NT)
                        v.tensor_scalar(ln_ve[:, :], ln_mv[:, :, 1], LN_EPS, None, ALU.add).then_inc(s_lnve, 1)
                    if s == 11 and pre:
                        dve.wait_ge(s_ln, q1 + 1)
                        v.tensor_tensor(dt[:, p1, :, :], dt[:, p1, :, :], xb[:, :, :], ALU.max).then_inc(s_dt, 1)
                    if s == 12 and pre:
                        need(dve, s_split, q1 * 5)
                        jw = await_filled(dve, b, k, "dn")
                        v.scalar_tensor_tensor(out=bprod[:, :], in0=work[0:XP_ROWS, jw, 0:T], scalar=bn_rows[:, 0:1],
                                               in1=xp[:, :], op0=ALU.add, op1=ALU.mult).then_inc(emptied[jw], 1)
                    if s == 15 and post:
                        par = img_par(b, -1 if k == 0 else 0)
                        kc = (k - 1) % K
                        for h in range(CH):
                            jw = await_filled(dve, b, k, f"wo{h}")
                            xs = img[:, par, h, kc * T:(kc + 1) * T]
                            v.scalar_tensor_tensor(out=xs, in0=work[:, jw, 0:T], scalar=bo[:, h:h + 1],
                                                   in1=xs, op0=ALU.add, op1=ALU.add).then_inc(emptied[jw], 1)
                        for h in range(CH):
                            await_emptied(dve, b, k, f"wo{h}")
                            hold("dve", dve, b)
                            v.bn_stats(gn_st[1][:, h, kc * 6:kc * 6 + 6],
                                       img[:, par, h, kc * T:(kc + 1) * T]).then_inc(s_gst[1], 1)
                    if L1 in do and k in L1_CHUNKS:
                        if s == 9:
                            lif(b, k, L1_CHUNKS[k][0])
                        if s == 12:
                            lif(b, k, L1_CHUNKS[k][1])
                    if TIN in do and k in TIN_CHUNKS and s in (7, 13):
                        kc = TIN_CHUNKS[k][0 if s == 7 else 1]
                        for h in range(CH):
                            await_emptied(dve, b, k, f"ti{kc}_{h}")
                            hold("dve", dve, b)
                            v.bn_stats(gn_st[0][:, h, kc * 6:kc * 6 + 6],
                                       img[:, img_par(b, 1), h, kc * T:(kc + 1) * T]).then_inc(s_gst[0], 1)
                    if k == 4 and TIN in do:
                        if s == 13:
                            channel_means(0, b + 1)
                        if s == 14:
                            group_deviation(0, b + 1, b, k)
                        if s == 15:
                            group_variance(0, b, k)
                    if k == 1 and GN1 in do:
                        if s == 0:
                            channel_means(1, b - 1)
                        if s == 1:
                            group_deviation(1, b - 1, b, k)
                        if s == 2:
                            group_variance(1, b, k)
                    if k == 1 and s == 5 and GN1 in do:
                        jw = await_filled(dve, b, k, "b1")
                        v.tensor_tensor(b1s[:, :], work[:, jw, 0:CH], b1c[:, :], ALU.add).then_inc(emptied[jw], 1)

            walk(dve, iteration)

        @block.tensor
        def _(pe):
            t = nc.tensor
            pe.wait_ge(s_w1, 16)
            pe.wait_ge(s_set_pool, 2)
            for hi in range(CH):
                for ho in range(CH):
                    last = t.transpose(ht[:, 0, hi * C + ho * P:hi * C + (ho + 1) * P],
                                       w1s[:, ho, hi * P:(hi + 1) * P], ident[:, :])
            last.then_inc(s_setp, 1)
            pe.wait_ge(s_set_dve, 2)
            pe.wait_ge(s_set_pool, 4)

            def conv(b, k, c, lo, hi):
                i = turn(b, k, f"cv{c}")[0]
                if lo == 0:
                    await_emptied(pe, b, k, f"xh{c}")
                    claim(pe, b, k, f"cv{c}")
                for tap in range(lo, hi):
                    dy, dx = divmod(tap, 3)
                    last = t.matmul(work[:, i, 0:T].rearrange("p (r w) -> p r w", w=W), conv_diag[:, c, tap, :],
                                    xhp[:, c % 3, dy:dy + ROWS, dx:dx + W], start=tap == 0, stop=tap == TAPS - 1)
                if hi == TAPS:
                    last.then_inc(filled[i], 1)

            def iteration(b, k):
                do = does(b, k)
                q0, q1 = b * K + k - 1, b * K + k + 1
                k1 = (k + 1) % K
                p0, p1 = (k - 1) % 2, k1 % 2
                main, pre = "main" in do, PRE in do
                xn0, xn1 = (k - 1) % 3, k1 % 3
                for s in range(NS):
                    for c, lo, hi in CONV_PARTS.get(s, ()):
                        if pre and lo > 0:
                            conv(b, k, c, lo, hi)
                    for kind, name in groups(k, s):
                        if kind not in do:
                            continue
                        if name[:2] == "cv":
                            for part in CONV_PARTS[s]:
                                if part[0] == int(name[2]):
                                    conv(b, k, *part)
                            continue
                        i = claim(pe, b, k, name)
                        if name[:2] == "bb":
                            n = int(name[2:])
                            par = p1 if n < 2 else k % 2
                            if n < 2:
                                pe.wait_ge(s_split, q1 * 5 + 5)
                            last = t.matmul(work[:, i, 0:T], one_hot[:, n:n + 1].to_broadcast([XP_ROWS, P]),
                                            bparts[:, par, :], start=True, stop=True)
                        elif name[:2] == "xh":
                            c = int(name[2:])
                            pe.wait_ge(s_xn, q1 + 1)
                            if c == 0 and k1 == 0:
                                pe.wait_ge(s_edge, (b + 1) * 2 + 1)
                            if c == 0 and k1 == K - 1:
                                pe.wait_ge(s_edge, b * 2 + 2)
                            for h in range(CH):
                                last = t.matmul(work[:, i, 0:HALO], win[:, h, c * P:(c + 1) * P], xn[:, xn1, h, :],
                                                start=h == 0, stop=h == CH - 1)
                        elif name[0] == "z":
                            c = int(name[1:])
                            for h in range(CH):
                                last = t.matmul(work[:, i, 0:T], win[:, h, D + c * P:D + (c + 1) * P],
                                                xn[:, xn0, h, W:W + T], start=h == 0, stop=h == CH - 1)
                        elif name == "xp":
                            await_emptied(pe, b, k, f"cv{DC - 1}")
                            for c in range(DC):
                                last = t.matmul(work[0:XP_ROWS, i, 0:T], wxp[:, c, :], xc[:, p1, c, :],
                                                start=c == 0, stop=c == DC - 1)
                        elif name == "ct":
                            for m in range(NT):
                                for c in range(DC):
                                    last = t.matmul(work[:, i, m * NS:(m + 1) * NS], xc[:, p1, c, m * P:(m + 1) * P],
                                                    wx[:, c, RANK + NS:RANK + 2 * NS], start=c == 0, stop=c == DC - 1)
                        elif name[:2] == "dt":
                            c = int(name[2:])
                            await_emptied(pe, b, k, "xp")
                            last = t.matmul(work[:, i, 0:T], wdt[:, c * P:(c + 1) * P], xp[:, :], start=True, stop=True)
                        elif name == "dn":
                            pe.wait_ge(s_dt, q1 + 1)
                            for c in range(DC):
                                last = t.matmul(work[0:XP_ROWS, i, 0:T], wnp[:, c, :], dt[:, p1, c, :],
                                                start=c == 0, stop=c == DC - 1)
                        elif name[:2] == "bt":
                            c = int(name[2:])
                            pe.wait_ge(s_lnp, q0 * 6 + 6)
                            for m in range(NT):
                                last = t.transpose(work[:, i, m * P:(m + 1) * P], y[:, p0, m, c * P:(c + 1) * P],
                                                   ident[:, :])
                        elif name[:2] == "wo":
                            h = int(name[2:])
                            for c in range(DC):
                                pe.wait_ge(s_yz, q0 * DC + c + 1)
                                last = t.matmul(work[:, i, 0:T], wo[:, c, h * P:(h + 1) * P], zs[:, c, :],
                                                start=c == 0, stop=c == DC - 1)
                        elif name[:2] == "yi":
                            m = int(name[2:])
                            for c in range(DC):
                                last = t.matmul(work[:, i, c * P:(c + 1) * P], xc[:, p1, c, m * P:(m + 1) * P],
                                                skip_diag[:, c, :], start=True, stop=True)
                        elif name[:2] == "ti":
                            kc, h = int(name[2]), int(name[4])
                            pe.wait_ge(s_xin, ((b + 1) * K + kc + 1) * 16)
                            for m in range(NT):
                                last = t.transpose(work[:, i, m * P:(m + 1) * P], xin[:, m, h * P:(h + 1) * P],
                                                   ident[:, :])
                        elif name[0] == "l":
                            kc, h = int(name[1]), int(name[3])
                            pe.wait_ge(s_w1s, b)
                            for hi in range(CH):
                                last = t.matmul(work[:, i, 0:T], w1s[:, hi, h * P:(h + 1) * P],
                                                img[:, img_par(b, -1), hi, kc * T:(kc + 1) * T],
                                                start=hi == 0, stop=hi == CH - 1)
                        elif name[:2] == "to":
                            kc, half = int(name[2]), int(name[4])
                            pe.wait_ge(s_lif, ((b - 1) * K + kc) * 6 + 4)
                            for m in ((0, 1) if half == 0 else (2,)):
                                for h in range(CH):
                                    o = (m - 2 * half) * C + h * P
                                    last = t.transpose(work[:, i, o:o + P], ob[:, h, m * P:(m + 1) * P],
                                                       ident[:, :])
                        elif name == "b1":
                            pe.wait_ge(s_gpl[1], (b - 1) * 3 + 3)
                            for ho in range(CH):
                                for hi in range(CH):
                                    last = t.matmul(work[:, i, ho:ho + 1], w1t[:, hi, ho * P:(ho + 1) * P],
                                                    gn_nb[1][:, hi:hi + 1], start=hi == 0, stop=hi == CH - 1)
                        elif name[:2] == "gm":
                            w = int(name[2])
                            e = b + 1 if w == 0 else b - 1
                            pe.wait_ge(s_gag[w], e * CH + CH)
                            last = t.matmul(work[:, i, 0:CH], group_mean[:, :], gn_mv[w][:, :, 0], start=True, stop=True)
                        elif name[:2] == "gv":
                            w = int(name[2])
                            e = b + 1 if w == 0 else b - 1
                            pe.wait_ge(s_gdv[w], e * 3 + 3)
                            last = t.matmul(work[:, i, 0:CH], group_mean[:, :], gn_dv[w][:, :], start=True, stop=True)
                        last.then_inc(filled[i], 1)
                    if main:
                        i = (b * K + k) * NS + s
                        j = (k * NS + s) % 3
                        pe.wait_ge(s_scan, i + 1)
                        for m in range(NT):
                            need(pe, s_y, 3 * i + m - NHT + 1)
                            for c in range(DC):
                                last = t.transpose(ht[:, (3 * s + m) % NHT, c * P:(c + 1) * P],
                                                   st[:, j, c, m * P:(m + 1) * P], ident[:, :])
                            last.then_inc(s_ht, 1)

            walk(pe, iteration)


_INS = ['x', 'L0_conv_W_in', 'L0_conv_conv_k', 'L0_conv_W_xproj', 'L0_conv_W_dt', 'L0_conv_b_dt', 'L0_conv_A_log',
        'L0_conv_Dskip', 'L0_conv_W_dtN', 'L0_conv_b_dtN', 'L0_conv_ln_g', 'L0_conv_ln_b', 'L0_conv_W_out',
        'L0_conv_b_out', 'L1_conv_W', 'L1_conv_b']
_OUTS = [((B, H, W, C), 'float32')]


def kernel(**inputs):
    import numpy as _np
    import concourse.bacc as _bacc
    from concourse import mybir as _mybir
    from concourse.bass_utils import run_bass_kernel_spmd as _run

    nc = _bacc.Bacc("TRN2", target_bir_lowering=False, num_devices=1)
    arrays, args = {}, []
    for name in _INS:
        a = _np.ascontiguousarray(inputs[name])
        arrays[f"in_{name}_dram"] = a
        args.append(nc.dram_tensor(f"in_{name}_dram", a.shape, _mybir.dt.from_np(a.dtype), kind="ExternalInput").ap())
    for i, (shape, dtype) in enumerate(_OUTS):
        dt = _mybir.dt.from_np(_np.dtype(dtype))
        args.append(nc.dram_tensor(f"out_{i}_dram", shape, dt, kind="ExternalOutput").ap())
    vssm_lif_kernel(nc, *args)
    r = _run(nc, [arrays], core_ids=[0])
    got = tuple(r.results[0][f"out_{i}_dram"] for i in range(len(_OUTS)))
    return got[0]
```

```python
from contextlib import ExitStack

import concourse.bass as bass
from concourse import mybir

F32 = mybir.dt.float32
BF16 = mybir.dt.bfloat16
ALU = mybir.AluOpType
ACT = mybir.ActivationFunctionType

B, H, W, C = 8, 48, 48, 256
D, NS, RANK = 512, 16, 8
GROUP = 8
P = 128
CH, DC = C // P, D // P
ROWS = 8
T = ROWS * W
K = H // ROWS
NT = T // P
HW = H * W
HALO = (ROWS + 2) * W
WP = W + 2
TAPS = 9
LN_EPS = GN_EPS = 1e-5

PART_ROW = (0, 64, 96)
C_ROW = NS
DT_ROW = 32
XP_ROWS = PART_ROW[2] + NS

NWORK = 4
NHT = 4

PRE, POST, L1, TIN, GN1 = "pre", "post", "l1", "tin", "gn1"
L1_CHUNKS = {1: (0, 1), 2: (2, 3), 3: (4, 5)}
TIN_CHUNKS = {2: (0, 1), 3: (2, 3), 4: (4, 5)}
CONV_PARTS = {0: [(0, 0, 1)], 1: [(0, 1, 4)], 2: [(0, 4, 9)], 3: [(1, 0, 3)], 4: [(1, 3, 9)],
              5: [(2, 0, 6)], 6: [(2, 6, 9), (3, 0, 3)], 7: [(3, 3, 9)]}
CONV_BANK = NWORK - 1
AFTER_CONV = 8


def groups(k, s):
    out = []
    if s < 14:
        out.append(("main", f"bb{s + 2}"))
    out += {
        0: [(PRE, "xh0"), (PRE, "xh1")],
        1: [(PRE, "xh2")],
        3: [(PRE, "xh3")],
        8: [(PRE, "xp")],
        9: [(PRE, "ct")] + [(PRE, f"dt{c}") for c in range(DC)],
        10: [(POST, f"bt{c}") for c in range(DC)],
        11: [(POST, f"z{c}") for c in range(DC)],
        12: [(PRE, "dn")],
        13: [(POST, "wo0")],
        14: [(POST, "wo1"), (PRE, "bb0")],
        15: [(PRE, "bb1"), (PRE, "yi0"), (PRE, "yi1"), (PRE, "yi2")],
    }.get(s, [])
    if k in L1_CHUNKS:
        a, b = L1_CHUNKS[k]
        out += {8: [(L1, f"l{a}_0"), (L1, f"l{a}_1")], 10: [(L1, f"to{a}_0"), (L1, f"to{a}_1")],
                13: [(L1, f"l{b}_0"), (L1, f"l{b}_1")], 15: [(L1, f"to{b}_0"), (L1, f"to{b}_1")]}.get(s, [])
    if k in TIN_CHUNKS:
        a, b = TIN_CHUNKS[k]
        out += {9: [(TIN, f"ti{a}_0"), (TIN, f"ti{a}_1")], 12: [(TIN, f"ti{b}_0"), (TIN, f"ti{b}_1")]}.get(s, [])
    if k == 1:
        out += {1: [(GN1, "gm1")], 2: [(GN1, "gv1")], 4: [(GN1, "b1")]}.get(s, [])
    if k == 4:
        out += {14: [(TIN, "gm0")], 15: [(TIN, "gv0")]}.get(s, [])
    return out


def does(b, k):
    if not isinstance(b, int):
        return {"main", PRE, POST, L1, TIN, GN1}
    kinds = set()
    if 0 <= b < B:
        kinds.add("main")
    if 0 <= b * K + k + 1 < B * K:
        kinds.add(PRE)
    if 0 <= b * K + k - 1 < B * K:
        kinds.add(POST)
    if 1 <= b <= B:
        kinds |= {L1, GN1}
    if -1 <= b < B - 1:
        kinds.add(TIN)
    return kinds


def bank_turns():
    turns, fills = {}, [0] * NWORK
    for b in range(-1, B + 1):
        for k in range(K):
            n = 0
            for s in range(NS):
                for kind, name in groups(k, s):
                    if kind in does(b, k):
                        i = n % (CONV_BANK if s < AFTER_CONV else NWORK)
                        turns[b, k, name] = (i, fills[i])
                        fills[i] += 1
                    n += 1
                for c, lo, _ in CONV_PARTS.get(s, ()):
                    if lo == 0 and PRE in does(b, k):
                        turns[b, k, f"cv{c}"] = (CONV_BANK, fills[CONV_BANK])
                        fills[CONV_BANK] += 1
    return turns


TURNS = bank_turns()


def turn(b, k, name):
    back = 0
    while k < 0:
        k, back = k + K, back + 1
    if isinstance(b, int):
        return TURNS.get((b - back, k, name))
    known = {i: TURNS[i - back, k, name] for i in range(1, B - 1) if (i - back, k, name) in TURNS}
    bank, last = known[B - 2]
    growth = last - known[B - 3][1]
    assert all(known[i] == (bank, last - (B - 2 - i) * growth) for i in known)
    assert last - (B - 3) * growth >= 0
    return bank, b * growth + (last - (B - 2) * growth)


def vssm_lif_kernel(nc, x, w_in, conv_k, w_xproj, w_dt, b_dt, a_log, dskip, w_dtn, b_dtn, ln_g, ln_b,
                    w_out, b_out, w1, b1, out):
    ctx = ExitStack()
    with ctx:
        def sb(name, shape, dt=F32):
            return ctx.enter_context(nc.sbuf_tensor(name, shape, dt))

        def sem(name):
            return ctx.enter_context(nc.semaphore(name))

        ident = sb("ident", [P, P])
        group_mean = sb("group_mean", [P, P])
        win = sb("win", [P, CH, 2 * D])
        taps = sb("taps", [P, DC, TAPS])
        conv_diag = sb("conv_diag", [P, DC, TAPS, P])
        skip_diag = sb("skip_diag", [P, DC, P])
        skip = sb("skip", [P, DC])
        wx = sb("wx", [P, DC, RANK + 2 * NS])
        wxp = sb("wxp", [P, DC, XP_ROWS])
        wn = sb("wn", [P, DC, NS])
        wnp = sb("wnp", [P, DC, XP_ROWS])
        bn_rows = sb("bn_rows", [XP_ROWS, 1])
        wdt = sb("wdt", [XP_ROWS, D])
        bdt = sb("bdt", [P, DC])
        neg_a = sb("neg_a", [P, NS])
        a_raw = sb("a_raw", [P, NS])
        gamma = sb("gamma", [P, DC])
        beta = sb("beta", [P, DC])
        wo = sb("wo", [P, DC, C])
        bo = sb("bo", [P, CH])
        w1t = sb("w1t", [P, CH, C])
        w1s = sb("w1s", [P, CH, C])
        b1c = sb("b1c", [P, CH])
        b1s = sb("b1s", [P, CH])
        one_hot = sb("one_hot", [XP_ROWS, NS], BF16)
        half_neg = sb("half_neg", [P, 4])

        img = sb("img", [P, 2, CH, HW])
        volt = sb("volt", [P, CH, HW])
        xin = sb("xin", [P, NT, C])
        xn = sb("xn", [P, 3, CH, HALO])
        xhp = sb("xhp", [P, 3, ROWS + 2, WP])
        xc = sb("xc", [P, 2, DC, T])
        dt = sb("dt", [P, 2, DC, T])
        xb = sb("xb", [P, DC, T])
        xp = sb("xp", [XP_ROWS, T])
        ct = sb("ct", [P, 2, NT * NS])
        bprod = sb("bprod", [XP_ROWS, T])
        bparts = sb("bparts", [XP_ROWS, 2, T], BF16)
        bbc = sb("bbc", [P, 3, T])
        decay = sb("decay", [P, 2, DC, T])
        st = sb("st", [P, 3, DC, T])
        carry = sb("carry", [P, DC, NS])
        y = sb("y", [P, 2, NT, D])
        zs = xb
        ob = sb("ob", [P, CH, T])
        ot = sb("ot", [P, NT, C])
        ln_st = sb("ln_st", [P, NT, 6])
        ln_mv = sb("ln_mv", [P, NT, 2])
        ln_ve = sb("ln_ve", [P, NT])
        ln_rs = sb("ln_rs", [P, NT])
        ln_mr = sb("ln_mr", [P, NT])
        ln_nb = sb("ln_nb", [P, NT])
        gn_st = [sb(f"gn_st{w}", [P, CH, K * 6]) for w in range(2)]
        gn_mv = [sb(f"gn_mv{w}", [P, CH, 2]) for w in range(2)]
        gn_mu = [sb(f"gn_mu{w}", [P, CH]) for w in range(2)]
        gn_dm = [sb(f"gn_dm{w}", [P, CH]) for w in range(2)]
        gn_sq = [sb(f"gn_sq{w}", [P, CH]) for w in range(2)]
        gn_dv = [sb(f"gn_dv{w}", [P, CH]) for w in range(2)]
        gn_ve = [sb(f"gn_ve{w}", [P, CH]) for w in range(2)]
        gn_rs = [sb(f"gn_rs{w}", [P, CH]) for w in range(2)]
        gn_mr = [sb(f"gn_mr{w}", [P, CH]) for w in range(2)]
        gn_nb = [sb(f"gn_nb{w}", [P, CH]) for w in range(2)]

        work = ctx.enter_context(nc.psum_tensor("work", [P, NWORK, 512], F32))
        ht = ctx.enter_context(nc.psum_tensor("ht", [P, NHT, 512], F32))

        s_w = sem("weights_loaded")
        s_w1 = sem("w1_loaded")
        s_set_pool = sem("constants_by_pool")
        s_set_dve = sem("constants_by_dve")
        s_set_act = sem("constants_by_act")
        s_setp = sem("w1_transposed")
        filled = [sem(f"work_bank{i}_filled") for i in range(NWORK)]
        emptied = [sem(f"work_bank{i}_emptied") for i in range(NWORK)]
        s_xin = sem("x_tile_loaded")
        s_gst = [sem(f"gn{w}_stats") for w in range(2)]
        s_gag = [sem(f"gn{w}_channel_means") for w in range(2)]
        s_gdv = [sem(f"gn{w}_by_dve") for w in range(2)]
        s_gpl = [sem(f"gn{w}_scale_and_shift") for w in range(2)]
        s_xn = sem("xn_ready")
        s_exp = sem("dt_exp")
        s_ln = sem("dt_log")
        s_dt = sem("dt_ready")
        s_cast = sem("b_part_cast")
        s_rest = sem("b_rest_left")
        s_dec = sem("decay_ready")
        s_u = sem("scan_input_ready")
        s_scan = sem("scans_done")
        s_ht = sem("states_transposed")
        s_y = sem("y_accumulated")
        s_carry = sem("carry_saved")
        s_lnst = sem("ln_stats")
        s_lnmv = sem("ln_mean_var")
        s_lnve = sem("ln_var_eps")
        s_lnp = sem("ln_by_pool")
        s_yn = sem("y_normed")
        s_yz = sem("y_gated")
        s_w1s = sem("w1_scaled")
        s_lif = sem("lif_steps")
        s_out = sem("out_tile_stored")
        s_edge = sem("xn_edge_zeroed")
        s_hold = {e: sem(f"{e}_wait_held") for e in ("pool", "act", "dve")}

        block = ctx.enter_context(nc.Block())

        def need(eng, s, value):
            if not isinstance(value, int) or value > 0:
                eng.wait_ge(s, value)

        def hold(name, eng, b):
            if not isinstance(b, int):
                eng.sem_inc(s_hold[name], 1)

        def await_filled(eng, b, k, name):
            at = turn(b, k, name)
            if at is not None:
                eng.wait_ge(filled[at[0]], at[1] + 1)
                return at[0]

        def await_emptied(eng, b, k, name):
            at = turn(b, k, name)
            if at is not None:
                eng.wait_ge(emptied[at[0]], at[1] + 1)

        def claim(pe, b, k, name):
            i, before = turn(b, k, name)
            need(pe, emptied[i], before)
            return i

        def img_par(b, d=0):
            return (b + d + 2) % 2

        def walk(eng, iteration):
            for k in range(2, K):
                iteration(-1, k)
            for k in range(K):
                iteration(0, k)
            with eng.Fori(1, B - 1, 1) as b:
                for k in range(K):
                    iteration(b, k)
            for k in range(K):
                iteration(B - 1, k)
            for k in range(4):
                iteration(B, k)

        x_v = x.rearrange("b (k r) w c -> b k (r w) c", r=ROWS)
        out_v = out.rearrange("b (k r) w c -> b k (r w) c", r=ROWS)

        @block.sync
        def _(sp):
            def load(dst, src):
                sp.dma_start(dst, src, allow_slow_non_contiguous=True).then_inc(s_w, 16)

            def load_x(b, kc, d):
                before = {0: 4 - K, 1: 2, 2: 2, 3: 3, 4: 3, 5: 4}[kc]
                await_filled(sp, b, before, f"ti{(kc - 1) % K}_1")
                sp.dma_start(xin[:, :, :], x_v[b + d, kc].rearrange("(m p) c -> p m c", p=P)).then_inc(s_xin, 16)

            sp.sem_inc(s_out, 16)
            load_x(-1, 0, 1)
            load(win[:, :, :], w_in.rearrange("(h p) n -> p h n", p=P))
            for c in range(DC):
                sp.dma_start(taps[:, c, :], conv_k.rearrange("i j o d -> d (i j o)")[c * P:(c + 1) * P, :],
                             allow_slow_non_contiguous=True).then_inc(s_w, 16)
            load(wx[:, :, :], w_xproj.rearrange("(c p) n -> p c n", p=P))
            load(wn[:, :, :], w_dtn.rearrange("(c p) n -> p c n", p=P))
            load(wo[:, :, :], w_out.rearrange("(c p) n -> p c n", p=P))
            for v, t in ((b_dt, bdt), (dskip, skip), (ln_g, gamma), (ln_b, beta), (b_out, bo), (b1, b1c)):
                load(t[:, :], v.rearrange("(c p) -> p c", p=P))
            load(a_raw[:, :], a_log.rearrange("(o n) -> o n", o=1).to_broadcast([P, NS]))
            sp.dma_start(w1s[:, :, :], w1.rearrange("(h p) n -> p h n", p=P)).then_inc(s_w1, 16)
            sp.wait_ge(s_set_pool, 1)
            load(wdt[DT_ROW:DT_ROW + RANK, :], w_dt)
            for r in PART_ROW:
                load(bn_rows[r:r + NS, :], b_dtn.rearrange("(n o) -> n o", o=1))

            def store(b, kc):
                await_emptied(sp, b, {0: 1, 1: 1, 2: 2, 3: 2, 4: 3, 5: 3}[kc], f"to{kc}_1")
                sp.dma_start(out_v[b - 1, kc].rearrange("(m p) c -> p m c", p=P),
                             ot[:, :, :]).then_inc(s_out, 16)

            def iteration(b, k):
                do = does(b, k)
                tin = TIN_CHUNKS.get(k, ()) if TIN in do else ()
                l1 = L1_CHUNKS.get(k, ()) if L1 in do else ()
                for n in range(2):
                    if tin and not (isinstance(b, int) and b == -1 and tin[n] == 0):
                        load_x(b, tin[n], 1)
                    if l1:
                        store(b, l1[n])

            walk(sp, iteration)
            sp.wait_ge(s_out, B * K * 16 + 16)

        N_W = (1 + DC + 3 + 6 + 1 + 1 + 3) * 16

        @block.gpsimd
        def _(pool):
            g = nc.gpsimd
            g.memset(wdt[:, :], 0.0)
            g.memset(wxp[:, :, :], 0.0)
            g.memset(wnp[:, :, :], 0.0)
            g.memset(one_hot[:, :], 0.0)
            g.memset(half_neg[:, :], -0.5)
            g.memset(xhp[:, :, :, :], 0.0)
            g.memset(volt[:, :, :], 0.0)
            g.memset(ident[:, :], 0.0)
            g.memset(group_mean[:, :], 1.0 / GROUP)
            g.memset(bn_rows[:, :], 0.0).then_inc(s_set_pool, 1)
            pool.wait_ge(s_set_pool, 1)
            g.affine_select(out=ident[:, :], in_=ident[:, :], compare_op=ALU.not_equal, fill=1.0, base=0,
                            pattern=[[-1, P]], channel_multiplier=1)
            gm = group_mean[:, :].rearrange("p (g e) -> p g e", e=GROUP)
            g.affine_select(out=gm, in_=gm, compare_op=ALU.is_ge, fill=0.0, base=0,
                            pattern=[[-GROUP, P // GROUP], [0, GROUP]],
                            channel_multiplier=1).then_inc(s_set_pool, 1)
            pool.wait_ge(s_set_pool, 2)
            g.affine_select(out=gm, in_=gm, compare_op=ALU.is_ge, fill=0.0, base=GROUP - 1,
                            pattern=[[GROUP, P // GROUP], [0, GROUP]],
                            channel_multiplier=-1).then_inc(s_set_pool, 1)
            pool.wait_ge(s_w, N_W)
            pool.wait_ge(s_set_pool, 3)
            for c in range(DC):
                g.tensor_scalar(skip_diag[:, c, :], ident[:, :], skip[:, c:c + 1], None, ALU.mult)
                for t in range(TAPS):
                    last = g.tensor_scalar(conv_diag[:, c, t, :], ident[:, :], taps[:, c, t:t + 1], None, ALU.mult)
            last.then_inc(s_set_pool, 1)

            def scale_input(w, e, b, k):
                await_emptied(pool, b, k, f"gv{w}")
                g.tensor_tensor(gn_rs[w][:, :], gn_ve[w][:, :], half_neg[:, 0:CH], ALU.pow).then_inc(s_gpl[w], 1)
                pool.wait_ge(s_gpl[w], e * 3 + 1)
                g.tensor_tensor(gn_mr[w][:, :], gn_mu[w][:, :], gn_rs[w][:, :], ALU.mult).then_inc(s_gpl[w], 1)
                pool.wait_ge(s_gpl[w], e * 3 + 2)
                hold("pool", pool, b)
                g.tensor_scalar(gn_nb[w][:, :], gn_mr[w][:, :], -1.0, 0.0, ALU.mult, ALU.add).then_inc(s_gpl[w], 1)

            def zero_edges(b, k):
                k1 = (k + 1) % K
                if k1 in (0, K - 1):
                    await_filled(pool, b, k - 1, f"z{DC - 1}")
                    hold("pool", pool, b)
                    edge = slice(0, W) if k1 == 0 else slice(HALO - W, HALO)
                    g.memset(xn[:, k1 % 3, :, edge], 0.0).then_inc(s_edge, 1)

            def scan_input(b, k, n, ahead):
                kq = (k + ahead) % K
                i = (b * K + k + ahead) * NS + n
                j = (kq * NS + n) % 3
                await_emptied(pool, b, k - 1 if n == 1 else k, f"bb{n}")
                need(pool, s_ht, NT * (i - 2))
                back = 3 - n if n < 3 else 0
                kk = k + ahead - (1 if back else 0)
                if kk % K < K - 1:
                    images = b if kk >= 0 else b - 1
                    need(pool, s_carry, (images * (K - 1) + kk) * NS + (n - 3) % NS + 1)
                if n == 0:
                    await_emptied(pool, b, k, f"cv{DC - 1}")
                g.tensor_tensor(st[:, j, :, :], xc[:, kq % 2, :, :],
                                bbc[:, j, :].unsqueeze(1).to_broadcast([P, DC, T]),
                                ALU.mult).then_inc(s_u, 1)

            def split(b, k):
                q1 = b * K + k + 1
                par = (k + 1) % 2
                need(pool, s_u, q1 * NS - (1 if "main" in does(b, k) else 0))
                for part, r0 in enumerate(PART_ROW[1:]):
                    pool.wait_ge(s_cast, q1 * 3 + part + 1)
                    g.tensor_tensor(bprod[r0:XP_ROWS, :], bprod[r0:XP_ROWS, :], bparts[r0:XP_ROWS, par, :],
                                    ALU.subtract).then_inc(s_rest, 1)
                    pool.wait_ge(s_rest, q1 * 2 + part + 1)

            def iteration(b, k):
                do = does(b, k)
                q0 = b * K + k - 1
                p0 = (k - 1) % 2
                for s in range(NS):
                    if s == 0 and PRE in do:
                        zero_edges(b, k)
                    if s < NS - 1 and "main" in do:
                        scan_input(b, k, s + 1, 0)
                    if s == NS - 1 and PRE in do:
                        scan_input(b, k, 0, 1)
                    if s == 1 and POST in do:
                        pool.wait_ge(s_lnve, q0 + 1)
                        g.tensor_tensor(ln_rs[:, :], ln_ve[:, :], half_neg[:, 0:NT], ALU.pow).then_inc(s_lnp, 1)
                        pool.wait_ge(s_lnp, q0 * 3 + 1)
                        g.tensor_tensor(ln_mr[:, :], ln_mv[:, :, 0], ln_rs[:, :], ALU.mult).then_inc(s_lnp, 1)
                        pool.wait_ge(s_lnp, q0 * 3 + 2)
                        hold("pool", pool, b)
                        g.tensor_scalar(ln_nb[:, :], ln_mr[:, :], -1.0, 0.0, ALU.mult, ALU.add).then_inc(s_lnp, 1)
                    if s == 12 and POST in do:
                        yg = y[:, p0, :, :].rearrange("p m d -> p (m d)").rearrange("p (c t) -> p c t", c=DC)
                        for c in range(DC):
                            await_emptied(pool, b, k, f"z{c}")
                            await_emptied(pool, b, k, f"bt{c}")
                            g.tensor_tensor(zs[:, c, :], zs[:, c, :], yg[:, c, :], ALU.mult).then_inc(s_yz, 1)
                    if s == 13 and PRE in do:
                        split(b, k)
                    if s == 15 and k == 4 and TIN in do:
                        scale_input(0, b + 1, b, k)
                    if s == 3 and k == 1 and GN1 in do:
                        await_filled(pool, b, 1 - K, "b1")
                        pool.wait_ge(s_setp, 1)
                        await_filled(pool, b, 3 - K, "l5_1")
                        scale_input(1, b - 1, b, k)
                        pool.wait_ge(s_gpl[1], (b - 1) * 3 + 3)
                        hold("pool", pool, b)
                        for h in range(CH):
                            last = g.tensor_scalar(w1s[:, h, :], w1t[:, h, :], gn_rs[1][:, h:h + 1], 0.0,
                                                   ALU.mult, ALU.add)
                        last.then_inc(s_w1s, 1)

            walk(pool, iteration)

        @block.scalar
        def _(act):
            a = nc.scalar
            TABLES = "natural_log_exp_and_others"
            a.preload_act_table_set(TABLES)
            act.wait_ge(s_w, N_W)
            a.activation(neg_a[:, :], a_raw[:, :], ACT.Exp).then_inc(s_set_act, 1)

            def iteration(b, k):
                do = does(b, k)
                q0, q1 = b * K + k - 1, b * K + k + 1
                k1 = (k + 1) % K
                p0, p1 = (k - 1) % 2, k1 % 2
                main, pre, post = "main" in do, PRE in do, POST in do

                def bank_copy(name, dst, cols, rows=P, view=lambda v: v, func=ACT.Copy, **kw):
                    i = await_filled(act, b, k, name)
                    if name[:2] == "ti":
                        hold("act", act, b)
                    a.activation(dst, view(work[0:rows, i, 0:cols]), func, **kw).then_inc(emptied[i], 1)

                def next_decay():
                    n = (s + 1) % NS
                    if (main if s < NS - 1 else pre):
                        ahead = 1 if s == NS - 1 else 0
                        qn = b * K + k + ahead
                        i = qn * NS + n
                        need(act, s_scan, i - 1)
                        if n == 0:
                            act.wait_ge(s_dt, qn + 1)
                            if isinstance(b, int) and b == -1:
                                act.wait_ge(s_set_dve, 3)
                        a.activation(decay[:, n % 2, :, :], dt[:, (k + ahead) % 2, :, :], ACT.Exp,
                                     scale=neg_a[:, n:n + 1]).then_inc(s_dec, 1)

                for s in range(NS):
                    if s == 0 and pre:
                        d = 1 if k == K - 1 else 0
                        act.wait_ge(s_gpl[0], (b + d) * 3 + 3)
                        await_filled(act, b, k - 1, f"z{DC - 1}")
                        hold("act", act, b)
                        lo = k1 * T - W
                        r0, r1 = (W if k1 == 0 else 0), (HALO - W if k1 == K - 1 else HALO)
                        for h in range(CH):
                            last = a.activation(xn[:, k1 % 3, h, r0:r1], img[:, img_par(b, d), h, lo + r0:lo + r1],
                                                ACT.Identity, bias=gn_nb[0][:, h:h + 1], scale=gn_rs[0][:, h:h + 1])
                        last.then_inc(s_xn, 1)
                    if main and s < NS - 2:
                        pass
                    else:
                        next_decay()
                    silu = False
                    for kind, name in groups(k, s):
                        if kind not in do:
                            continue
                        if name[:2] == "bb":
                            n = int(name[2:])
                            i = (q1 if n < 2 else q1 - 1) * NS + n
                            need(act, s_u, i - 2)
                            kq = k1 if n < 2 else k
                            bank_copy(name, bbc[:, (kq * NS + n) % 3, :], T)
                            if n > 1:
                                next_decay()
                        elif name[:2] == "xh":
                            c = int(name[2:])
                            if c == 0:
                                await_filled(act, b, k - 1, "cv3")
                            if c == 1:
                                await_filled(act, b, k - 1, "cv1")
                            if c == 2:
                                await_filled(act, b, k - 1, "cv2")
                            if c == 3:
                                await_filled(act, b, k, "cv0")
                            bank_copy(name, xhp[:, c % 3, :, 1:1 + W], HALO,
                                          view=lambda v: v.rearrange("p (r w) -> p r w", w=W))
                        elif name == "xp":
                            await_emptied(act, b, k - 1, "dn")
                            bank_copy(name, xp[:, :], T, XP_ROWS)
                        elif name == "ct":
                            need(act, s_y, (q1 - 1) * NS * NT)
                            bank_copy(name, ct[:, p1, :].rearrange("p (m n) -> p m n", m=NT), NT * XP_ROWS,
                                      view=lambda v: v.rearrange("p (m r) -> p m r", m=NT)[:, :, C_ROW:C_ROW + NS])
                        elif name[:2] == "dt":
                            c = int(name[2:])
                            if c == 0:
                                await_filled(act, b, k - 1, "wo1")
                            i = await_filled(act, b, k, name)
                            a.activation(xb[:, c, :], work[:, i, 0:T], ACT.Identity, bias=bdt[:, c:c + 1])
                            a.activation(dt[:, p1, c, :], work[:, i, 0:T], ACT.Abs,
                                         bias=bdt[:, c:c + 1]).then_inc(emptied[i], 1)
                        elif name[:2] == "bt":
                            c = int(name[2:])
                            yg = y[:, p0, :, :].rearrange("p m d -> p (m d)").rearrange("p (c t) -> p c t", c=DC)
                            await_filled(act, b, k, f"bt{DC - 1}")
                            bank_copy(name, yg[:, c, :], T, func=ACT.Identity,
                                          bias=beta[:, c:c + 1], scale=gamma[:, c:c + 1])
                        elif name[0] == "z":
                            c = int(name[1:])
                            if c == 0:
                                if pre:
                                    act.wait_ge(s_dt, q1 + 1)
                                else:
                                    await_filled(act, b, k - 1, "wo1")
                            bank_copy(name, zs[:, c, :], T, func=ACT.Silu)
                            silu = True
                        elif name[:2] == "yi":
                            m = int(name[2:])
                            need(act, s_yz, (q1 - 1) * DC)
                            bank_copy(name, y[:, p1, m, :], D)
                        elif name[:2] == "ti":
                            kc, h = int(name[2]), int(name[4])
                            if not (isinstance(b, int) and b < 1):
                                act.wait_ge(s_lif, ((b - 1) * K + kc) * 6 + 6)
                            bank_copy(name, img[:, img_par(b, 1), h, kc * T:(kc + 1) * T], T)
                        elif name[:2] == "to":
                            kc, half = int(name[2]), int(name[4])
                            if half == 0:
                                act.wait_ge(s_out, ((b - 1) * K + kc) * 16 + 16)
                            dst = ot[:, 0:2, :] if half == 0 else ot[:, 2:3, :]
                            n = 2 if half == 0 else 1
                            bank_copy(name, dst, n * C, view=lambda v, n=n: v.rearrange("p (m c) -> p m c", m=n))
                    if silu:
                        a.preload_act_table_set(TABLES)
                    for c, _, hi in CONV_PARTS.get(s, ()):
                        if hi == TAPS and pre:
                            if c == 0:
                                need(act, s_u, (q1 - 1) * NS)
                            bank_copy(f"cv{c}", xc[:, p1, c, :], T)
                    if s == 2 and post:
                        act.wait_ge(s_lnp, q0 * 3 + 3)
                        for m in range(NT):
                            a.activation(y[:, p0, m, :], y[:, p0, m, :], ACT.Identity, bias=ln_nb[:, m:m + 1],
                                         scale=ln_rs[:, m:m + 1]).then_inc(s_yn, 1)
                    if s == 9 and pre:
                        await_emptied(act, b, k, f"dt{DC - 1}")
                        a.activation(dt[:, p1, :, :], dt[:, p1, :, :], ACT.Exp, scale=-1.0).then_inc(s_exp, 1)
                    if s == 10 and pre:
                        act.wait_ge(s_exp, q1 + 1)
                        a.activation(dt[:, p1, :, :], dt[:, p1, :, :], ACT.Ln, bias=1.0).then_inc(s_ln, 1)
                    if s == 13 and pre:
                        await_emptied(act, b, k, "dn")
                        await_filled(act, b, k - 1, f"bb{NS - 1}")
                        for part, row in enumerate(PART_ROW):
                            if part > 0:
                                act.wait_ge(s_rest, q1 * 2 + part)
                            a.activation(bparts[row:XP_ROWS, p1, :], bprod[row:XP_ROWS, :],
                                         ACT.Copy).then_inc(s_cast, 1)

            walk(act, iteration)

        @block.vector
        def _(dve):
            v = nc.vector
            dve.wait_ge(s_w, N_W)
            dve.wait_ge(s_set_pool, 3)
            r1, r2, r3 = PART_ROW
            for r in PART_ROW:
                v.tensor_copy(wxp[:, :, r:r + NS], wx[:, :, RANK:RANK + NS])
                v.tensor_copy(wnp[:, :, r:r + NS], wn[:, :, :])
                v.tensor_copy(one_hot[r:r + NS, :], ident[r:r + NS, r:r + NS])
            v.tensor_copy(wxp[:, :, C_ROW:C_ROW + NS], wx[:, :, RANK + NS:RANK + 2 * NS])
            v.tensor_copy(wxp[:, :, DT_ROW:DT_ROW + RANK], wx[:, :, 0:RANK]).then_inc(s_set_dve, 1)
            dve.wait_ge(s_setp, 1)
            v.tensor_copy(w1t[:, :, :].rearrange("p h n -> p (h n)"), ht[:, 0, :]).then_inc(s_set_dve, 1)
            dve.wait_ge(s_set_act, 1)
            dve.wait_ge(s_set_dve, 2)
            v.tensor_scalar(neg_a[:, :], neg_a[:, :], -1.0, None, ALU.mult).then_inc(s_set_dve, 1)

            def channel_means(w, e):
                dve.wait_ge(s_gst[w], (e + 1) * CH * K)
                hold("dve", dve, e)
                for h in range(CH):
                    v.bn_aggr(gn_mv[w][:, h, :], gn_st[w][:, h, :]).then_inc(s_gag[w], 1)

            def group_deviation(w, e, b, k):
                i = await_filled(dve, b, k, f"gm{w}")
                v.tensor_copy(gn_mu[w][:, :], work[:, i, 0:CH]).then_inc(emptied[i], 1)
                await_emptied(dve, b, k, f"gm{w}")
                v.tensor_tensor(gn_dm[w][:, :], gn_mv[w][:, :, 0], gn_mu[w][:, :], ALU.subtract).then_inc(s_gdv[w], 1)
                dve.wait_ge(s_gdv[w], e * 3 + 1)
                v.tensor_tensor(gn_sq[w][:, :], gn_dm[w][:, :], gn_dm[w][:, :], ALU.mult).then_inc(s_gdv[w], 1)
                dve.wait_ge(s_gdv[w], e * 3 + 2)
                v.tensor_tensor(gn_dv[w][:, :], gn_sq[w][:, :], gn_mv[w][:, :, 1], ALU.add).then_inc(s_gdv[w], 1)

            def group_variance(w, b, k):
                i = await_filled(dve, b, k, f"gv{w}")
                v.tensor_scalar(gn_ve[w][:, :], work[:, i, 0:CH], GN_EPS, None, ALU.add).then_inc(emptied[i], 1)

            def lif(b, k, kc):
                il = (b - 1) * K + kc
                par = img_par(b, -1)
                cols = slice(kc * T, (kc + 1) * T)
                if kc == 0:
                    await_emptied(dve, b, 1, "b1")
                await_filled(dve, b, {0: 3 - K, 1: 1, 2: 1, 3: 2, 4: 2, 5: 3}[kc], f"to{(kc - 1) % K}_1")
                for h in range(CH):
                    i = await_filled(dve, b, k, f"l{kc}_{h}")
                    v.scalar_tensor_tensor(out=ob[:, h, :], in0=work[:, i, 0:T], scalar=b1s[:, h:h + 1],
                                           in1=volt[:, h, cols], op0=ALU.add, op1=ALU.subtract).then_inc(emptied[i], 1)
                for h in range(CH):
                    await_emptied(dve, b, k, f"l{kc}_{h}")
                    v.scalar_tensor_tensor(out=volt[:, h, cols], in0=ob[:, h, :], scalar=0.5,
                                           in1=volt[:, h, cols], op0=ALU.mult, op1=ALU.add).then_inc(s_lif, 1)
                for h in range(CH):
                    dve.wait_ge(s_lif, il * 6 + 1 + h)
                    v.scalar_tensor_tensor(out=ob[:, h, :], in0=volt[:, h, cols], scalar=1.0,
                                           in1=img[:, par, h, cols], op0=ALU.is_ge, op1=ALU.add).then_inc(s_lif, 1)
                for h in range(CH):
                    v.scalar_tensor_tensor(out=volt[:, h, cols], in0=volt[:, h, cols], scalar=1.0,
                                           in1=volt[:, h, cols], op0=ALU.is_lt, op1=ALU.mult).then_inc(s_lif, 1)

            def accumulate(b, k, n, before):
                kq = (k - before) % K
                q = b * K + k - before
                i = q * NS + n
                for m in range(NT):
                    dve.wait_ge(s_ht, 3 * i + m + 1)
                    if n == 0:
                        if m == 0:
                            await_emptied(dve, b, k - 1, "ct")
                        await_emptied(dve, b, k - 1, f"yi{m}")
                    else:
                        dve.wait_ge(s_y, 3 * (i - 1) + m + 1)
                    j = (3 * n + m) % NHT
                    v.scalar_tensor_tensor(out=y[:, kq % 2, m, :], in0=ht[:, j, :],
                                           scalar=ct[:, kq % 2, m * NS + n:m * NS + n + 1],
                                           in1=y[:, kq % 2, m, :], op0=ALU.mult, op1=ALU.add).then_inc(s_y, 1)

            def iteration(b, k):
                do = does(b, k)
                q0, q1 = b * K + k - 1, b * K + k + 1
                k1 = (k + 1) % K
                p0, p1 = (k - 1) % 2, k1 % 2
                main, pre, post = "main" in do, PRE in do, POST in do
                for s in range(NS):
                    i = (b * K + k) * NS + s
                    j = (k * NS + s) % 3
                    if main:
                        dve.wait_ge(s_dec, i + 1)
                        dve.wait_ge(s_u, i + 1)
                        if k > 0:
                            dve.wait_ge(s_carry, (b * (K - 1) + k - 1) * NS + s + 1)
                        for c in range(DC):
                            first = 0.0 if k == 0 else carry[:, c, s:s + 1]
                            last = v.tensor_tensor_scan(st[:, j, c, :], decay[:, s % 2, c, :], st[:, j, c, :],
                                                        first, ALU.mult, ALU.add)
                        last.then_inc(s_scan, 1)
                    if s > 0 and main:
                        accumulate(b, k, s - 1, 0)
                    if s == 0 and post:
                        accumulate(b, k, NS - 1, 1)
                    if main and k < K - 1:
                        dve.wait_ge(s_scan, i + 1)
                        v.tensor_copy(carry[:, :, s], st[:, j, :, T - 1]).then_inc(s_carry, 1)
                    if s == 0 and post:
                        for m in range(NT):
                            dve.wait_ge(s_y, (q0 * NS + NS - 1) * 3 + m + 1)
                            v.bn_stats(ln_st[:, m, :], y[:, p0, m, :]).then_inc(s_lnst, 1)
                        for m in range(NT):
                            dve.wait_ge(s_lnst, q0 * NT + m + 1)
                            hold("dve", dve, b)
                            v.bn_aggr(ln_mv[:, m, :], ln_st[:, m, :]).then_inc(s_lnmv, 1)
                        dve.wait_ge(s_lnmv, q0 * NT + NT)
                        v.tensor_scalar(ln_ve[:, :], ln_mv[:, :, 1], LN_EPS, None, ALU.add).then_inc(s_lnve, 1)
                    if s == 10 and pre:
                        dve.wait_ge(s_ln, q1 + 1)
                        v.scalar_tensor_tensor(out=dt[:, p1, :, :], in0=xb[:, :, :], scalar=0.0, in1=dt[:, p1, :, :],
                                               op0=ALU.max, op1=ALU.add).then_inc(s_dt, 1)
                    if s == 12 and pre:
                        need(dve, s_cast, q1 * 3)
                        jw = await_filled(dve, b, k, "dn")
                        v.scalar_tensor_tensor(out=bprod[:, :], in0=work[0:XP_ROWS, jw, 0:T], scalar=bn_rows[:, 0:1],
                                               in1=xp[:, :], op0=ALU.add, op1=ALU.mult).then_inc(emptied[jw], 1)
                    if s in (13, 14) and post:
                        h = s - 13
                        jw = await_filled(dve, b, k, f"wo{h}")
                        xs = img[:, img_par(b, -1 if k == 0 else 0), h, (k - 1) % K * T:((k - 1) % K + 1) * T]
                        v.scalar_tensor_tensor(out=xs, in0=work[:, jw, 0:T], scalar=bo[:, h:h + 1],
                                               in1=xs, op0=ALU.add, op1=ALU.add).then_inc(emptied[jw], 1)
                    if s in (14, 15) and post:
                        h, kc = s - 14, (k - 1) % K
                        await_emptied(dve, b, k, f"wo{h}")
                        hold("dve", dve, b)
                        v.bn_stats(gn_st[1][:, h, kc * 6:kc * 6 + 6],
                                   img[:, img_par(b, -1 if k == 0 else 0), h, kc * T:(kc + 1) * T]).then_inc(s_gst[1], 1)
                    if L1 in do and k in L1_CHUNKS:
                        if s == 8:
                            lif(b, k, L1_CHUNKS[k][0])
                        if s == 13:
                            lif(b, k, L1_CHUNKS[k][1])
                    if TIN in do and k in TIN_CHUNKS and s in (11, 13):
                        kc = TIN_CHUNKS[k][0 if s == 11 else 1]
                        for h in range(CH):
                            await_emptied(dve, b, k, f"ti{kc}_{h}")
                            hold("dve", dve, b)
                            v.bn_stats(gn_st[0][:, h, kc * 6:kc * 6 + 6],
                                       img[:, img_par(b, 1), h, kc * T:(kc + 1) * T]).then_inc(s_gst[0], 1)
                    if k == 4 and TIN in do:
                        if s == 13:
                            channel_means(0, b + 1)
                        if s == 14:
                            group_deviation(0, b + 1, b, k)
                        if s == 15:
                            group_variance(0, b, k)
                    if k == 1 and GN1 in do:
                        if s == 0:
                            channel_means(1, b - 1)
                        if s == 1:
                            group_deviation(1, b - 1, b, k)
                        if s == 2:
                            group_variance(1, b, k)
                    if k == 1 and s == 5 and GN1 in do:
                        jw = await_filled(dve, b, k, "b1")
                        v.tensor_tensor(b1s[:, :], work[:, jw, 0:CH], b1c[:, :], ALU.add).then_inc(emptied[jw], 1)

            walk(dve, iteration)

        @block.tensor
        def _(pe):
            t = nc.tensor
            pe.wait_ge(s_w1, 16)
            pe.wait_ge(s_set_pool, 2)
            for hi in range(CH):
                for ho in range(CH):
                    last = t.transpose(ht[:, 0, hi * C + ho * P:hi * C + (ho + 1) * P],
                                       w1s[:, ho, hi * P:(hi + 1) * P], ident[:, :])
            last.then_inc(s_setp, 1)
            pe.wait_ge(s_set_dve, 2)
            pe.wait_ge(s_set_pool, 4)

            def conv(b, k, c, lo, hi):
                i = turn(b, k, f"cv{c}")[0]
                if lo == 0:
                    await_emptied(pe, b, k, f"xh{c}")
                    claim(pe, b, k, f"cv{c}")
                for tap in range(lo, hi):
                    dy, dx = divmod(tap, 3)
                    last = t.matmul(work[:, i, 0:T].rearrange("p (r w) -> p r w", w=W), conv_diag[:, c, tap, :],
                                    xhp[:, c % 3, dy:dy + ROWS, dx:dx + W], start=tap == 0, stop=tap == TAPS - 1)
                if hi == TAPS:
                    last.then_inc(filled[i], 1)

            def iteration(b, k):
                do = does(b, k)
                q0, q1 = b * K + k - 1, b * K + k + 1
                k1 = (k + 1) % K
                p0, p1 = (k - 1) % 2, k1 % 2
                main, pre = "main" in do, PRE in do
                xn0, xn1 = (k - 1) % 3, k1 % 3
                for s in range(NS):
                    for kind, name in groups(k, s):
                        if kind not in do:
                            continue
                        i = claim(pe, b, k, name)
                        if name[:2] == "bb":
                            n = int(name[2:])
                            par = p1 if n < 2 else k % 2
                            if n < 2:
                                pe.wait_ge(s_cast, q1 * 3 + 3)
                            last = t.matmul(work[:, i, 0:T], one_hot[:, n:n + 1].to_broadcast([XP_ROWS, P]),
                                            bparts[:, par, :], start=True, stop=True)
                        elif name[:2] == "xh":
                            c = int(name[2:])
                            pe.wait_ge(s_xn, q1 + 1)
                            if c == 0 and k1 == 0:
                                pe.wait_ge(s_edge, (b + 1) * 2 + 1)
                            if c == 0 and k1 == K - 1:
                                pe.wait_ge(s_edge, b * 2 + 2)
                            for h in range(CH):
                                last = t.matmul(work[:, i, 0:HALO], win[:, h, c * P:(c + 1) * P], xn[:, xn1, h, :],
                                                start=h == 0, stop=h == CH - 1)
                        elif name[0] == "z":
                            c = int(name[1:])
                            for h in range(CH):
                                last = t.matmul(work[:, i, 0:T], win[:, h, D + c * P:D + (c + 1) * P],
                                                xn[:, xn0, h, W:W + T], start=h == 0, stop=h == CH - 1)
                        elif name == "xp":
                            await_emptied(pe, b, k, f"cv{DC - 1}")
                            for c in range(DC):
                                last = t.matmul(work[0:XP_ROWS, i, 0:T], wxp[:, c, :], xc[:, p1, c, :],
                                                start=c == 0, stop=c == DC - 1)
                        elif name == "ct":
                            await_emptied(pe, b, k, "xp")
                            for m in range(NT):
                                last = t.transpose(work[:, i, m * XP_ROWS:(m + 1) * XP_ROWS], xp[:, m * P:(m + 1) * P],
                                                   ident[0:XP_ROWS, 0:XP_ROWS])
                        elif name[:2] == "dt":
                            c = int(name[2:])
                            await_emptied(pe, b, k, "xp")
                            last = t.matmul(work[:, i, 0:T], wdt[:, c * P:(c + 1) * P], xp[:, :], start=True, stop=True)
                        elif name == "dn":
                            pe.wait_ge(s_dt, q1 + 1)
                            for c in range(DC):
                                last = t.matmul(work[0:XP_ROWS, i, 0:T], wnp[:, c, :], dt[:, p1, c, :],
                                                start=c == 0, stop=c == DC - 1)
                        elif name[:2] == "bt":
                            c = int(name[2:])
                            pe.wait_ge(s_yn, q0 * NT + NT)
                            for m in range(NT):
                                last = t.transpose(work[:, i, m * P:(m + 1) * P], y[:, p0, m, c * P:(c + 1) * P],
                                                   ident[:, :])
                        elif name[:2] == "wo":
                            h = int(name[2:])
                            for c in range(DC):
                                pe.wait_ge(s_yz, q0 * DC + c + 1)
                                last = t.matmul(work[:, i, 0:T], wo[:, c, h * P:(h + 1) * P], zs[:, c, :],
                                                start=c == 0, stop=c == DC - 1)
                        elif name[:2] == "yi":
                            m = int(name[2:])
                            for c in range(DC):
                                last = t.matmul(work[:, i, c * P:(c + 1) * P], xc[:, p1, c, m * P:(m + 1) * P],
                                                skip_diag[:, c, :], start=True, stop=True)
                        elif name[:2] == "ti":
                            kc, h = int(name[2]), int(name[4])
                            pe.wait_ge(s_xin, ((b + 1) * K + kc + 1) * 16)
                            for m in range(NT):
                                last = t.transpose(work[:, i, m * P:(m + 1) * P], xin[:, m, h * P:(h + 1) * P],
                                                   ident[:, :])
                        elif name[0] == "l":
                            kc, h = int(name[1]), int(name[3])
                            pe.wait_ge(s_w1s, b)
                            for hi in range(CH):
                                last = t.matmul(work[:, i, 0:T], w1s[:, hi, h * P:(h + 1) * P],
                                                img[:, img_par(b, -1), hi, kc * T:(kc + 1) * T],
                                                start=hi == 0, stop=hi == CH - 1)
                        elif name[:2] == "to":
                            kc, half = int(name[2]), int(name[4])
                            pe.wait_ge(s_lif, ((b - 1) * K + kc) * 6 + 4)
                            for m in ((0, 1) if half == 0 else (2,)):
                                for h in range(CH):
                                    o = (m - 2 * half) * C + h * P
                                    last = t.transpose(work[:, i, o:o + P], ob[:, h, m * P:(m + 1) * P],
                                                       ident[:, :])
                        elif name == "b1":
                            pe.wait_ge(s_gpl[1], (b - 1) * 3 + 3)
                            for ho in range(CH):
                                for hi in range(CH):
                                    last = t.matmul(work[:, i, ho:ho + 1], w1t[:, hi, ho * P:(ho + 1) * P],
                                                    gn_nb[1][:, hi:hi + 1], start=hi == 0, stop=hi == CH - 1)
                        elif name[:2] == "gm":
                            w = int(name[2])
                            e = b + 1 if w == 0 else b - 1
                            pe.wait_ge(s_gag[w], e * CH + CH)
                            last = t.matmul(work[:, i, 0:CH], group_mean[:, :], gn_mv[w][:, :, 0], start=True, stop=True)
                        elif name[:2] == "gv":
                            w = int(name[2])
                            e = b + 1 if w == 0 else b - 1
                            pe.wait_ge(s_gdv[w], e * 3 + 3)
                            last = t.matmul(work[:, i, 0:CH], group_mean[:, :], gn_dv[w][:, :], start=True, stop=True)
                        last.then_inc(filled[i], 1)
                    for part in CONV_PARTS.get(s, ()):
                        if pre:
                            conv(b, k, *part)
                    if main:
                        i = (b * K + k) * NS + s
                        j = (k * NS + s) % 3
                        pe.wait_ge(s_scan, i + 1)
                        for m in range(NT):
                            need(pe, s_y, 3 * i + m - NHT + 1)
                            for c in range(DC):
                                last = t.transpose(ht[:, (3 * s + m) % NHT, c * P:(c + 1) * P],
                                                   st[:, j, c, m * P:(m + 1) * P], ident[:, :])
                            last.then_inc(s_ht, 1)

            walk(pe, iteration)


_INS = ['x', 'L0_conv_W_in', 'L0_conv_conv_k', 'L0_conv_W_xproj', 'L0_conv_W_dt', 'L0_conv_b_dt', 'L0_conv_A_log',
        'L0_conv_Dskip', 'L0_conv_W_dtN', 'L0_conv_b_dtN', 'L0_conv_ln_g', 'L0_conv_ln_b', 'L0_conv_W_out',
        'L0_conv_b_out', 'L1_conv_W', 'L1_conv_b']
_OUTS = [((B, H, W, C), 'float32')]


def kernel(**inputs):
    import numpy as _np
    import concourse.bacc as _bacc
    from concourse import mybir as _mybir
    from concourse.bass_utils import run_bass_kernel_spmd as _run

    nc = _bacc.Bacc("TRN2", target_bir_lowering=False, num_devices=1)
    arrays, args = {}, []
    for name in _INS:
        a = _np.ascontiguousarray(inputs[name])
        arrays[f"in_{name}_dram"] = a
        args.append(nc.dram_tensor(f"in_{name}_dram", a.shape, _mybir.dt.from_np(a.dtype), kind="ExternalInput").ap())
    for i, (shape, dtype) in enumerate(_OUTS):
        dt = _mybir.dt.from_np(_np.dtype(dtype))
        args.append(nc.dram_tensor(f"out_{i}_dram", shape, dt, kind="ExternalOutput").ap())
    vssm_lif_kernel(nc, *args)
    r = _run(nc, [arrays], core_ids=[0])
    got = tuple(r.results[0][f"out_{i}_dram"] for i in range(len(_OUTS)))
    return got[0]
```

```python
from contextlib import ExitStack

import concourse.bass as bass
from concourse import mybir

F32 = mybir.dt.float32
BF16 = mybir.dt.bfloat16
ALU = mybir.AluOpType
ACT = mybir.ActivationFunctionType

B, H, W, C = 8, 48, 48, 256
D, NS, RANK = 512, 16, 8
GROUP = 8
P = 128
CH, DC = C // P, D // P
ROWS = 8
T = ROWS * W
K = H // ROWS
NT = T // P
HW = H * W
HALO = (ROWS + 2) * W
WP = W + 2
TAPS = 3
LN_EPS = GN_EPS = 1e-5

PART_ROW = (0, 64, 96)
C_ROW = NS
DT_ROW = 32
XP_ROWS = PART_ROW[2] + NS

NWORK = 4
NHT = 4

PRE, PRE2, POST, L1, TIN, GN1 = "pre", "pre2", "post", "l1", "tin", "gn1"
L1_CHUNKS = {1: (0,), 2: (1, 2), 3: (3, 4), 4: (5,)}
L1_AT = {kc: k for k, taken in L1_CHUNKS.items() for kc in taken}
TIN_CHUNKS = {2: (0, 1), 3: (2, 3), 4: (4, 5)}
Q = 32
NQ = P // Q
STEPS = NQ * 3
CONV_PARTS = {2: [(0, 0, STEPS)], 4: [(1, 0, STEPS)], 6: [(2, 0, STEPS)],
              7: [(3, 0, STEPS)]}
NBT = T * DC // 512
LIF_STEPS = ({"half": 9, "charge": 10, "fire": 11, "store": 12},
             {"half": 1, "charge": 2, "fire": 3, "store": 4},
             {"half": 4, "charge": 5, "fire": 6, "store": 7})
Y_LAG = 1
CONV_BANK = NWORK - 1
AFTER_CONV = 8


def lif_slots(k):
    return [(kc, step, slot) for n, kc in enumerate(L1_CHUNKS.get(k, ()))
            for step, slot in LIF_STEPS[0 if kc == 0 else n + 1].items()]


def groups(k, s):
    out = []
    if s < 14:
        out.append(("main", f"bb{s + 2}"))
    out += {
        0: [(PRE, "xh1")],
        1: [(PRE, "xh2")],
        3: [(PRE, "xh3")],
        6: [(POST, f"bt{g}") for g in range(NBT)],
        8: [(PRE, "xp")],
        9: [(PRE, "ct")] + [(PRE, f"dt{c}") for c in range(DC)],
        11: [(POST, f"z{c}") for c in range(DC)],
        12: [(PRE, "dn")],
        13: [(POST, "wo0")],
        14: [(POST, "wo1"), (PRE, "bb0")],
        15: [(PRE, "bb1"), (PRE, "yi0"), (PRE, "yi1"), (PRE, "yi2"), (PRE2, "xh0")],
    }.get(s, [])
    for kc, step, slot in lif_slots(k):
        if slot == s and step == "store":
            out += [(L1, f"to{kc}_0"), (L1, f"to{kc}_1")]
    if k in TIN_CHUNKS:
        a, b = TIN_CHUNKS[k]
        out += {8: [(TIN, f"ti{a}_0"), (TIN, f"ti{a}_1")], 10: [(TIN, f"ti{b}_0"), (TIN, f"ti{b}_1")]}.get(s, [])
    for kc, step, slot in lif_slots(k):
        if slot == s and step == "half":
            out.append((L1, f"l{kc}_0"))
        if slot == s and step == "charge":
            out.insert(1, (L1, f"l{kc}_1"))
    if k == 1:
        out += {1: [(GN1, "gm1")], 2: [(GN1, "gv1")], 4: [(GN1, "b1")]}.get(s, [])
    if k == 4:
        out += {12: [(TIN, "gm0")], 13: [(TIN, "gv0")]}.get(s, [])
    return out


def does(b, k):
    if not isinstance(b, int):
        return {"main", PRE, PRE2, POST, L1, TIN, GN1}
    kinds = set()
    if 0 <= b < B:
        kinds.add("main")
    if 0 <= b * K + k + 1 < B * K:
        kinds.add(PRE)
    if 0 <= b * K + k + 2 < B * K:
        kinds.add(PRE2)
    if 0 <= b * K + k - 1 < B * K:
        kinds.add(POST)
    if 1 <= b <= B:
        kinds |= {L1, GN1}
    if -1 <= b < B - 1:
        kinds.add(TIN)
    return kinds


def following(b, k):
    return (b, k + 1) if k < K - 1 else (b + 1, 0)


def bank_turns():
    turns, fills = {}, [0] * NWORK
    for b in range(-1, B + 1):
        for k in range(K):
            n = 0
            for s in range(NS):
                for kind, name in groups(k, s):
                    if kind in does(b, k):
                        i = n % (CONV_BANK if s < AFTER_CONV else NWORK)
                        at = following(b, k) if kind == PRE2 else (b, k)
                        turns[*at, name] = (i, fills[i])
                        fills[i] += 1
                    n += 1
                for c, lo, _ in CONV_PARTS.get(s, ()):
                    if lo == 0 and PRE in does(b, k):
                        turns[b, k, f"cv{c}"] = (CONV_BANK, fills[CONV_BANK])
                        fills[CONV_BANK] += 1
    return turns


TURNS = bank_turns()


def turn(b, k, name):
    back = 0
    while k < 0:
        k, back = k + K, back + 1
    if isinstance(b, int):
        return TURNS.get((b - back, k, name))
    known = {i: TURNS[i - back, k, name] for i in range(1, B - 1) if (i - back, k, name) in TURNS}
    bank, last = known[B - 2]
    growth = last - known[B - 3][1]
    assert all(known[i] == (bank, last - (B - 2 - i) * growth) for i in known)
    assert last - (B - 3) * growth >= 0
    return bank, b * growth + (last - (B - 2) * growth)


def vssm_lif_kernel(nc, x, w_in, conv_k, w_xproj, w_dt, b_dt, a_log, dskip, w_dtn, b_dtn, ln_g, ln_b,
                    w_out, b_out, w1, b1, out):
    ctx = ExitStack()
    with ctx:
        def sb(name, shape, dt=F32):
            return ctx.enter_context(nc.sbuf_tensor(name, shape, dt))

        def sem(name):
            return ctx.enter_context(nc.semaphore(name))

        ident = sb("ident", [P, P])
        group_mean = sb("group_mean", [P, P])
        win = sb("win", [P, CH, 2 * D])
        taps = sb("taps", [TAPS * Q, DC * NQ, TAPS])
        unit = sb("unit", [TAPS * Q, Q])
        conv_w = sb("conv_w", [TAPS * Q, DC * NQ, TAPS, Q])
        skip_diag = sb("skip_diag", [P, DC, P])
        skip = sb("skip", [P, DC])
        wxp = sb("wxp", [P, DC, XP_ROWS])
        wnp = sb("wnp", [P, DC, XP_ROWS])
        bn_rows = sb("bn_rows", [XP_ROWS, 1])
        wdt = sb("wdt", [XP_ROWS, D])
        bdt = sb("bdt", [P, DC])
        neg_a = sb("neg_a", [P, NS])
        a_raw = sb("a_raw", [P, NS])
        gamma = sb("gamma", [P, DC])
        beta = sb("beta", [P, DC])
        wo = sb("wo", [P, DC, C])
        bo = sb("bo", [P, CH])
        w1t = sb("w1t", [P, CH, C])
        w1s = sb("w1s", [P, CH, C])
        b1c = sb("b1c", [P, CH])
        b1s = sb("b1s", [P, CH])
        one_hot = sb("one_hot", [XP_ROWS, NS], BF16)
        half_neg = sb("half_neg", [P, 4])

        img = sb("img", [P, 2, CH, HW])
        volt = sb("volt", [P, CH, HW])
        xin = sb("xin", [P, NT, C])
        xn = sb("xn", [P, 3, CH, HALO])
        xhp = sb("xhp", [P, 3, ROWS + 2, WP])
        tri = sb("tri", [TAPS * Q, 2, NQ, ROWS, WP])
        xc = sb("xc", [P, 2, DC, T])
        dt = sb("dt", [P, 2, DC, T])
        xb = sb("xb", [P, DC, T])
        xp = sb("xp", [XP_ROWS, T])
        ct = sb("ct", [P, 2, NT * NS])
        bprod = sb("bprod", [XP_ROWS, T])
        bparts = sb("bparts", [XP_ROWS, 2, T], BF16)
        bbc = sb("bbc", [P, 3, T])
        decay = sb("decay", [P, 2, DC, 1 + T])
        st = sb("st", [P, 3, DC, 1 + T])
        carry = sb("carry", [P, DC, NS])
        y = sb("y", [P, 2, NT, D])
        wx = y[:, 0, 0, 0:DC * (RANK + 2 * NS)].rearrange("p (c n) -> p c n", c=DC)
        wn = y[:, 0, 1, 0:DC * NS].rearrange("p (c n) -> p c n", c=DC)
        zs = xb
        ob = sb("ob", [P, CH, T])
        ot = sb("ot", [P, NT, C])
        ln_st = sb("ln_st", [P, NT, 6])
        ln_mv = sb("ln_mv", [P, NT, 2])
        ln_ve = sb("ln_ve", [P, NT])
        ln_rs = sb("ln_rs", [P, NT])
        ln_mr = sb("ln_mr", [P, NT])
        ln_nb = sb("ln_nb", [P, NT])
        gn_st = [sb(f"gn_st{w}", [P, CH, K * 6]) for w in range(2)]
        gn_mv = [sb(f"gn_mv{w}", [P, CH, 2]) for w in range(2)]
        gn_mu = [sb(f"gn_mu{w}", [P, CH]) for w in range(2)]
        gn_dm = [sb(f"gn_dm{w}", [P, CH]) for w in range(2)]
        gn_sq = [sb(f"gn_sq{w}", [P, CH]) for w in range(2)]
        gn_dv = [sb(f"gn_dv{w}", [P, CH]) for w in range(2)]
        gn_ve = [sb(f"gn_ve{w}", [P, CH]) for w in range(2)]
        gn_rs = [sb(f"gn_rs{w}", [P, CH]) for w in range(2)]
        gn_mr = [sb(f"gn_mr{w}", [P, CH]) for w in range(2)]
        gn_nb = [sb(f"gn_nb{w}", [P, CH]) for w in range(2)]

        work = ctx.enter_context(nc.psum_tensor("work", [P, NWORK, 512], F32))
        ht = ctx.enter_context(nc.psum_tensor("ht", [P, NHT, 512], F32))

        s_w = sem("weights_loaded")
        s_w1 = sem("w1_loaded")
        s_set_pool = sem("constants_by_pool")
        s_set_dve = sem("constants_by_dve")
        s_set_act = sem("constants_by_act")
        s_setp = sem("w1_transposed")
        filled = [sem(f"work_bank{i}_filled") for i in range(NWORK)]
        emptied = [sem(f"work_bank{i}_emptied") for i in range(NWORK)]
        s_xin = sem("x_tile_loaded")
        s_gst = [sem(f"gn{w}_stats") for w in range(2)]
        s_gag = [sem(f"gn{w}_channel_means") for w in range(2)]
        s_gdv = [sem(f"gn{w}_by_dve") for w in range(2)]
        s_gpl = [sem(f"gn{w}_scale_and_shift") for w in range(2)]
        s_xn = sem("xn_ready")
        s_tri = [sem(f"xh{c}_rows_copied") for c in range(DC)]
        s_exp = sem("dt_exp")
        s_ln = sem("dt_log")
        s_dt = sem("dt_ready")
        s_cast = sem("b_part_cast")
        s_rest = sem("b_rest_left")
        s_dec = sem("decay_ready")
        s_u = sem("scan_input_ready")
        s_scan = sem("scans_done")
        s_ht = sem("states_transposed")
        s_y = sem("y_accumulated")
        s_carry = sem("carry_saved")
        s_lnst = sem("ln_stats")
        s_lnmv = sem("ln_mean_var")
        s_lnve = sem("ln_var_eps")
        s_lnp = sem("ln_by_pool")
        s_yn = sem("y_normed")
        s_yz = sem("y_gated")
        s_w1s = sem("w1_scaled")
        s_volt = sem("membrane_steps")
        s_spike = sem("spikes_added")
        s_out = sem("out_tile_stored")
        s_edge = sem("xn_edge_zeroed")
        s_hold = {e: sem(f"{e}_wait_held") for e in ("pool", "act", "dve", "sp")}

        block = ctx.enter_context(nc.Block())

        def need(eng, s, value):
            if not isinstance(value, int) or value > 0:
                eng.wait_ge(s, value)

        def hold(name, eng, b):
            if not isinstance(b, int):
                eng.sem_inc(s_hold[name], 1)

        def await_filled(eng, b, k, name):
            at = turn(b, k, name)
            if at is not None:
                eng.wait_ge(filled[at[0]], at[1] + 1)
                return at[0]

        def await_emptied(eng, b, k, name):
            at = turn(b, k, name)
            if at is not None:
                eng.wait_ge(emptied[at[0]], at[1] + 1)

        def claim(pe, b, k, name):
            i, before = turn(b, k, name)
            need(pe, emptied[i], before)
            return i

        def img_par(b, d=0):
            return (b + d + 2) % 2

        def walk(eng, iteration):
            for k in range(2, K):
                iteration(-1, k)
            for k in range(K):
                iteration(0, k)
            with eng.Fori(1, B - 1, 1) as b:
                for k in range(K):
                    iteration(b, k)
            for k in range(K):
                iteration(B - 1, k)
            for k in range(L1_AT[K - 1] + 1):
                iteration(B, k)

        x_v = x.rearrange("b (k r) w c -> b k (r w) c", r=ROWS)
        out_v = out.rearrange("b (k r) w c -> b k (r w) c", r=ROWS)

        @block.sync
        def _(sp):
            def load(dst, src):
                sp.dma_start(dst, src, allow_slow_non_contiguous=True).then_inc(s_w, 16)

            def load_x(b, kc, d):
                before = {0: 4 - K, 1: 2, 2: 2, 3: 3, 4: 3, 5: 4}[kc]
                await_filled(sp, b, before, f"ti{(kc - 1) % K}_1")
                sp.dma_start(xin[:, :, :], x_v[b + d, kc].rearrange("(m p) c -> p m c", p=P)).then_inc(s_xin, 16)

            sp.sem_inc(s_out, 16)
            load_x(-1, 0, 1)
            load(win[:, :, :], w_in.rearrange("(h p) n -> p h n", p=P))
            for dy in range(TAPS):
                for dx in range(TAPS):
                    load(taps[dy * Q:(dy + 1) * Q, :, dx], conv_k[dy, dx, 0, :].rearrange("(g i) -> i g", i=Q))
            load(wx[:, :, :], w_xproj.rearrange("(c p) n -> p c n", p=P))
            load(wn[:, :, :], w_dtn.rearrange("(c p) n -> p c n", p=P))
            load(wo[:, :, :], w_out.rearrange("(c p) n -> p c n", p=P))
            for v, t in ((b_dt, bdt), (dskip, skip), (ln_g, gamma), (ln_b, beta), (b_out, bo), (b1, b1c)):
                load(t[:, :], v.rearrange("(c p) -> p c", p=P))
            load(a_raw[:, :], a_log.rearrange("(o n) -> o n", o=1).to_broadcast([P, NS]))
            sp.dma_start(w1s[:, :, :], w1.rearrange("(h p) n -> p h n", p=P)).then_inc(s_w1, 16)
            sp.wait_ge(s_set_pool, 1)
            load(wdt[DT_ROW:DT_ROW + RANK, :], w_dt)
            for r in PART_ROW:
                load(bn_rows[r:r + NS, :], b_dtn.rearrange("(n o) -> n o", o=1))

            def store(b, kc):
                await_emptied(sp, b, L1_AT[kc], f"to{kc}_1")
                sp.dma_start(out_v[b - 1, kc].rearrange("(m p) c -> p m c", p=P),
                             ot[:, :, :]).then_inc(s_out, 16)

            def copy_rows(b, k, c):
                await_emptied(sp, b, k, f"xh{c}")
                hold("sp", sp, b)
                await_filled(sp, b, k if c > 1 else k - 1, f"cv{(c - 2) % DC}")
                hold("sp", sp, b)
                for g in range(NQ):
                    for dy in range(TAPS):
                        sp.dma_start(tri[dy * Q:(dy + 1) * Q, c % 2, g, :, :],
                                     xhp[g * Q:(g + 1) * Q, c % 3, dy:dy + ROWS, :]).then_inc(s_tri[c], 16)

            def iteration(b, k):
                do = does(b, k)
                tin = TIN_CHUNKS.get(k, ()) if TIN in do else ()
                l1 = L1_CHUNKS.get(k, ()) if L1 in do else ()
                if PRE in do:
                    for c in range(DC):
                        copy_rows(b, k, c)
                for kc in l1:
                    store(b, kc)
                for kc in tin:
                    if not (isinstance(b, int) and b == -1 and kc == 0):
                        load_x(b, kc, 1)

            walk(sp, iteration)
            sp.wait_ge(s_out, B * K * 16 + 16)

        N_W = (1 + TAPS * TAPS + 3 + 6 + 1 + 1 + 3) * 16

        @block.gpsimd
        def _(pool):
            g = nc.gpsimd
            g.memset(wdt[:, :], 0.0)
            g.memset(wxp[:, :, :], 0.0)
            g.memset(wnp[:, :, :], 0.0)
            g.memset(one_hot[:, :], 0.0)
            g.memset(half_neg[:, :], -0.5)
            g.memset(xhp[:, :, :, :], 0.0)
            g.memset(volt[:, :, :], 0.0)
            for j in range(2):
                g.memset(decay[:, j, :, 0], 0.0)
            g.memset(ident[:, :], 0.0)
            g.memset(group_mean[:, :], 1.0 / GROUP)
            g.memset(bn_rows[:, :], 0.0).then_inc(s_set_pool, 1)
            pool.wait_ge(s_set_pool, 1)
            g.affine_select(out=ident[:, :], in_=ident[:, :], compare_op=ALU.not_equal, fill=1.0, base=0,
                            pattern=[[-1, P]], channel_multiplier=1)
            gm = group_mean[:, :].rearrange("p (g e) -> p g e", e=GROUP)
            g.affine_select(out=gm, in_=gm, compare_op=ALU.is_ge, fill=0.0, base=0,
                            pattern=[[-GROUP, P // GROUP], [0, GROUP]],
                            channel_multiplier=1).then_inc(s_set_pool, 1)
            pool.wait_ge(s_set_pool, 2)
            g.affine_select(out=gm, in_=gm, compare_op=ALU.is_ge, fill=0.0, base=GROUP - 1,
                            pattern=[[GROUP, P // GROUP], [0, GROUP]],
                            channel_multiplier=-1).then_inc(s_set_pool, 1)
            pool.wait_ge(s_w, N_W)
            pool.wait_ge(s_set_pool, 3)
            for c in range(DC):
                g.tensor_scalar(skip_diag[:, c, :], ident[:, :], skip[:, c:c + 1], None, ALU.mult)
            pool.wait_ge(s_set_dve, 1)
            g.tensor_tensor(conv_w[:, :, :, :].rearrange("p g t j -> p (g t) j"),
                            unit[:, :].unsqueeze(1).to_broadcast([TAPS * Q, DC * NQ * TAPS, Q]),
                            taps[:, :, :].rearrange("p g t -> p (g t)").unsqueeze(2)
                            .to_broadcast([TAPS * Q, DC * NQ * TAPS, Q]), ALU.mult).then_inc(s_set_pool, 1)

            def scale_input(w, e, b, k):
                await_emptied(pool, b, k, f"gv{w}")
                g.tensor_tensor(gn_rs[w][:, :], gn_ve[w][:, :], half_neg[:, 0:CH], ALU.pow).then_inc(s_gpl[w], 1)
                pool.wait_ge(s_gpl[w], e * 3 + 1)
                g.tensor_tensor(gn_mr[w][:, :], gn_mu[w][:, :], gn_rs[w][:, :], ALU.mult).then_inc(s_gpl[w], 1)
                pool.wait_ge(s_gpl[w], e * 3 + 2)
                hold("pool", pool, b)
                g.tensor_scalar(gn_nb[w][:, :], gn_mr[w][:, :], -1.0, 0.0, ALU.mult, ALU.add).then_inc(s_gpl[w], 1)

            def zero_edges(b, k):
                k1 = (k + 1) % K
                if k1 in (0, K - 1):
                    await_filled(pool, b, k - 1, f"z{DC - 1}")
                    hold("pool", pool, b)
                    edge = slice(0, W) if k1 == 0 else slice(HALO - W, HALO)
                    g.memset(xn[:, k1 % 3, :, edge], 0.0).then_inc(s_edge, 1)

            def scan_input(b, k, n, ahead):
                kq = (k + ahead) % K
                i = (b * K + k + ahead) * NS + n
                j = (kq * NS + n) % 3
                await_emptied(pool, b, k - 1 if n == 1 else k, f"bb{n}")
                need(pool, s_ht, NT * (i - 2))
                if n == 0:
                    await_emptied(pool, b, k, f"cv{DC - 1}")
                back = 3 - n if n < 3 else 0
                kk = k + ahead - (1 if back else 0)
                if kk % K < K - 1:
                    images = b if kk >= 0 else b - 1
                    need(pool, s_carry, (images * (K - 1) + kk) * NS + (n - 3) % NS + 1)
                elif kq > 0:
                    pool.wait_ge(s_carry, ((b + (k + ahead) // K) * (K - 1) + kq - 1) * NS + n + 1)
                g.tensor_tensor(st[:, j, :, 1:], xc[:, kq % 2, :, :],
                                bbc[:, j, :].unsqueeze(1).to_broadcast([P, DC, T]), ALU.mult)
                if kq > 0:
                    g.tensor_copy(st[:, j, :, 0], carry[:, :, n]).then_inc(s_u, 1)
                else:
                    g.memset(st[:, j, :, 0], 0.0).then_inc(s_u, 1)

            def save_carry(b, k, n):
                pool.wait_ge(s_scan, (b * K + k) * NS + n + 1)
                hold("pool", pool, b)
                g.tensor_copy(carry[:, :, n], st[:, (k * NS + n) % 3, :, T]).then_inc(s_carry, 1)

            def split(b, k):
                q1 = b * K + k + 1
                par = (k + 1) % 2
                need(pool, s_u, q1 * NS - (1 if "main" in does(b, k) else 0))
                if "main" in does(b, k) and k < K - 1:
                    pool.wait_ge(s_carry, (b * (K - 1) + k) * NS + 13)
                for part, r0 in enumerate(PART_ROW[1:]):
                    pool.wait_ge(s_cast, q1 * 3 + part + 1)
                    g.tensor_tensor(bprod[r0:XP_ROWS, :], bprod[r0:XP_ROWS, :], bparts[r0:XP_ROWS, par, :],
                                    ALU.subtract).then_inc(s_rest, 1)
                    pool.wait_ge(s_rest, q1 * 2 + part + 1)

            def iteration(b, k):
                do = does(b, k)
                q0 = b * K + k - 1
                p0 = (k - 1) % 2
                for s in range(NS):
                    if s < NS - 1 and "main" in do:
                        scan_input(b, k, s + 1, 0)
                    if s == NS - 1 and PRE in do:
                        scan_input(b, k, 0, 1)
                    if "main" in do:
                        if s > 0 and k < K - 1:
                            save_carry(b, k, s - 1)
                        if s == 0 and k > 0:
                            save_carry(b, k - 1, NS - 1)
                    if s == Y_LAG and POST in do:
                        pool.wait_ge(s_lnve, q0 + 1)
                        g.tensor_tensor(ln_rs[:, :], ln_ve[:, :], half_neg[:, 0:NT], ALU.pow).then_inc(s_lnp, 1)
                        pool.wait_ge(s_lnp, q0 * 3 + 1)
                        g.tensor_tensor(ln_mr[:, :], ln_mv[:, :, 0], ln_rs[:, :], ALU.mult).then_inc(s_lnp, 1)
                        pool.wait_ge(s_lnp, q0 * 3 + 2)
                        hold("pool", pool, b)
                        g.tensor_scalar(ln_nb[:, :], ln_mr[:, :], -1.0, 0.0, ALU.mult, ALU.add).then_inc(s_lnp, 1)
                    if s == 12 and POST in do:
                        yg = y[:, p0, :, :].rearrange("p m d -> p (m d)").rearrange("p (c t) -> p c t", c=DC)
                        for c in range(DC):
                            await_emptied(pool, b, k, f"z{c}")
                            await_emptied(pool, b, k, f"bt{((c + 1) * T - 1) // 512}")
                            g.tensor_tensor(zs[:, c, :], zs[:, c, :], yg[:, c, :], ALU.mult).then_inc(s_yz, 1)
                    if s == 13 and PRE in do:
                        split(b, k)
                    if s == 14 and k == 4 and TIN in do:
                        scale_input(0, b + 1, b, k)
                    if s == 14 and PRE2 in do:
                        zero_edges(*following(b, k))
                    if s == 3 and k == 1 and GN1 in do:
                        await_filled(pool, b, 1 - K, "b1")
                        pool.wait_ge(s_setp, 1)
                        await_filled(pool, b, L1_AT[K - 1] - K, f"l{K - 1}_1")
                        scale_input(1, b - 1, b, k)
                        pool.wait_ge(s_gpl[1], (b - 1) * 3 + 3)
                        hold("pool", pool, b)
                        for h in range(CH):
                            last = g.tensor_scalar(w1s[:, h, :], w1t[:, h, :], gn_rs[1][:, h:h + 1], 0.0,
                                                   ALU.mult, ALU.add)
                        last.then_inc(s_w1s, 1)

            walk(pool, iteration)

        @block.scalar
        def _(act):
            a = nc.scalar
            TABLES = "natural_log_exp_and_others"
            a.preload_act_table_set(TABLES)
            act.wait_ge(s_w, N_W)
            a.activation(neg_a[:, :], a_raw[:, :], ACT.Exp).then_inc(s_set_act, 1)

            def iteration(b, k):
                do = does(b, k)
                q0, q1 = b * K + k - 1, b * K + k + 1
                k1 = (k + 1) % K
                p0, p1 = (k - 1) % 2, k1 % 2
                main, pre, post = "main" in do, PRE in do, POST in do

                def bank_copy(name, dst, cols, rows=P, view=lambda v: v, func=ACT.Copy, **kw):
                    i = await_filled(act, b, k, name)
                    if name[:2] == "ti":
                        hold("act", act, b)
                    a.activation(dst, view(work[0:rows, i, 0:cols]), func, **kw).then_inc(emptied[i], 1)

                def next_decay():
                    n = (s + 1) % NS
                    if (main if s < NS - 1 else pre):
                        ahead = 1 if s == NS - 1 else 0
                        qn = b * K + k + ahead
                        i = qn * NS + n
                        need(act, s_scan, i - 1)
                        if n == 0:
                            act.wait_ge(s_dt, qn + 1)
                            if isinstance(b, int) and b == -1:
                                act.wait_ge(s_set_dve, 3)
                        a.activation(decay[:, n % 2, :, 1:], dt[:, (k + ahead) % 2, :, :], ACT.Exp,
                                     scale=neg_a[:, n:n + 1]).then_inc(s_dec, 1)

                def evacuate_conv(s):
                    for c, _, hi in CONV_PARTS.get(s, ()):
                        if hi == STEPS:
                            if c == 0:
                                need(act, s_u, (q1 - 1) * NS)
                            bank_copy(f"cv{c}", xc[:, p1, c, :], T)

                def exp_and_log():
                    await_emptied(act, b, k, f"dt{DC - 1}")
                    a.activation(dt[:, p1, :, :], dt[:, p1, :, :], ACT.Exp, scale=-1.0).then_inc(s_exp, 1)
                    act.wait_ge(s_exp, q1 + 1)
                    a.activation(dt[:, p1, :, :], dt[:, p1, :, :], ACT.Ln, bias=1.0).then_inc(s_ln, 1)

                for s in range(NS):
                    if s == NS - 1 and PRE2 in do:
                        bx, kx = following(*following(b, k))
                        act.wait_ge(s_gpl[0], bx * 3 + 3)
                        await_filled(act, b, k, f"z{DC - 1}")
                        hold("act", act, b)
                        lo = kx * T - W
                        r0, r1 = (W if kx == 0 else 0), (HALO - W if kx == K - 1 else HALO)
                        for h in range(CH):
                            last = a.activation(xn[:, kx % 3, h, r0:r1],
                                                img[:, img_par(b, 0 if k < K - 2 else 1), h, lo + r0:lo + r1],
                                                ACT.Identity, bias=gn_nb[0][:, h:h + 1], scale=gn_rs[0][:, h:h + 1])
                        last.then_inc(s_xn, 1)
                    next_decay()
                    if pre and s > 0:
                        evacuate_conv(s - 1)
                    if s == Y_LAG + 1 and post:
                        act.wait_ge(s_lnp, q0 * 3 + 3)
                        for m in range(NT):
                            a.activation(y[:, p0, m, :], y[:, p0, m, :], ACT.Identity, bias=ln_nb[:, m:m + 1],
                                         scale=ln_rs[:, m:m + 1]).then_inc(s_yn, 1)
                    silu = False
                    if s == 10 and pre and not main:
                        exp_and_log()
                    for kind, name in groups(k, s):
                        if kind not in do:
                            continue
                        if name[:2] == "bb":
                            n = int(name[2:])
                            i = (q1 if n < 2 else q1 - 1) * NS + n
                            need(act, s_u, i - 2)
                            kq = k1 if n < 2 else k
                            bank_copy(name, bbc[:, (kq * NS + n) % 3, :], T)
                            if s == 10 and pre:
                                exp_and_log()
                        elif name[:2] == "xh":
                            c = int(name[2:])
                            bc, kc = following(b, k) if kind == PRE2 else (b, k)
                            qc = bc * K + kc + 1
                            before = {0: 3, 1: 1, 2: 2, 3: 0}[c]
                            need(act, s_tri[before], (qc + (c == 3)) * STEPS * 16)
                            i = await_filled(act, bc, kc, name)
                            a.activation(xhp[:, c % 3, :, 1:1 + W],
                                         work[:, i, 0:HALO].rearrange("p (r w) -> p r w", w=W),
                                         ACT.Copy).then_inc(emptied[i], 1)
                        elif name == "xp":
                            await_emptied(act, b, k - 1, "dn")
                            bank_copy(name, xp[:, :], T, XP_ROWS)
                        elif name == "ct":
                            need(act, s_y, (q1 - 1) * NS * NT)
                            bank_copy(name, ct[:, p1, :].rearrange("p (m n) -> p m n", m=NT), NT * XP_ROWS,
                                      view=lambda v: v.rearrange("p (m r) -> p m r", m=NT)[:, :, C_ROW:C_ROW + NS])
                        elif name[:2] == "dt":
                            c = int(name[2:])
                            if c == 0:
                                await_filled(act, b, k - 1, "wo1")
                            i = await_filled(act, b, k, name)
                            a.activation(xb[:, c, :], work[:, i, 0:T], ACT.Identity, bias=bdt[:, c:c + 1])
                            a.activation(dt[:, p1, c, :], work[:, i, 0:T], ACT.Abs,
                                         bias=bdt[:, c:c + 1]).then_inc(emptied[i], 1)
                        elif name[:2] == "bt":
                            yg = y[:, p0, :, :].rearrange("p m d -> p (m d)")
                            await_filled(act, b, k, f"bt{NBT - 1}")
                            i = await_filled(act, b, k, name)
                            lo = int(name[2:]) * 512
                            cuts = sorted({lo, lo + 512} | {c * T for c in range(DC) if lo < c * T < lo + 512})
                            for u0, u1 in zip(cuts, cuts[1:]):
                                c = u0 // T
                                last = a.activation(yg[:, u0:u1], work[:, i, u0 - lo:u1 - lo], ACT.Identity,
                                                    bias=beta[:, c:c + 1], scale=gamma[:, c:c + 1])
                            last.then_inc(emptied[i], 1)
                        elif name[0] == "z":
                            c = int(name[1:])
                            if c == 0:
                                if pre:
                                    act.wait_ge(s_dt, q1 + 1)
                                else:
                                    await_filled(act, b, k - 1, "wo1")
                            bank_copy(name, zs[:, c, :], T, func=ACT.Silu)
                            silu = True
                        elif name[:2] == "yi":
                            m = int(name[2:])
                            need(act, s_yz, (q1 - 1) * DC)
                            bank_copy(name, y[:, p1, m, :], D)
                        elif name[:2] == "ti":
                            kc, h = int(name[2]), int(name[4])
                            if not (isinstance(b, int) and b < 1):
                                act.wait_ge(s_spike, ((b - 1) * K + kc) * CH + CH)
                            bank_copy(name, img[:, img_par(b, 1), h, kc * T:(kc + 1) * T], T)
                        elif name[:2] == "to":
                            kc, half = int(name[2]), int(name[4])
                            if half == 0:
                                act.wait_ge(s_out, ((b - 1) * K + kc) * 16 + 16)
                            dst = ot[:, 0:2, :] if half == 0 else ot[:, 2:3, :]
                            n = 2 if half == 0 else 1
                            bank_copy(name, dst, n * C, view=lambda v, n=n: v.rearrange("p (m c) -> p m c", m=n))
                    if silu:
                        a.preload_act_table_set(TABLES)
                    if s == 13 and pre:
                        await_emptied(act, b, k, "dn")
                        await_filled(act, b, k - 1, f"bb{NS - 1}")
                        for part, row in enumerate(PART_ROW):
                            if part > 0:
                                act.wait_ge(s_rest, q1 * 2 + part)
                            a.activation(bparts[row:XP_ROWS, p1, :], bprod[row:XP_ROWS, :],
                                         ACT.Copy).then_inc(s_cast, 1)

            walk(act, iteration)

        @block.vector
        def _(dve):
            v = nc.vector
            dve.wait_ge(s_w, N_W)
            dve.wait_ge(s_set_pool, 3)
            r1, r2, r3 = PART_ROW
            for r in PART_ROW:
                v.tensor_copy(wxp[:, :, r:r + NS], wx[:, :, RANK:RANK + NS])
                v.tensor_copy(wnp[:, :, r:r + NS], wn[:, :, :])
                v.tensor_copy(one_hot[r:r + NS, :], ident[r:r + NS, r:r + NS])
            for dy in range(TAPS):
                v.tensor_copy(unit[dy * Q:(dy + 1) * Q, :], ident[dy * Q:(dy + 1) * Q, dy * Q:(dy + 1) * Q])
            v.tensor_copy(wxp[:, :, C_ROW:C_ROW + NS], wx[:, :, RANK + NS:RANK + 2 * NS])
            v.tensor_copy(wxp[:, :, DT_ROW:DT_ROW + RANK], wx[:, :, 0:RANK]).then_inc(s_set_dve, 1)
            dve.wait_ge(s_setp, 1)
            v.tensor_copy(w1t[:, :, :].rearrange("p h n -> p (h n)"), ht[:, 0, :]).then_inc(s_set_dve, 1)
            dve.wait_ge(s_set_act, 1)
            dve.wait_ge(s_set_dve, 2)
            v.tensor_scalar(neg_a[:, :], neg_a[:, :], -1.0, None, ALU.mult).then_inc(s_set_dve, 1)

            def channel_means(w, e):
                dve.wait_ge(s_gst[w], (e + 1) * CH * K)
                hold("dve", dve, e)
                for h in range(CH):
                    v.bn_aggr(gn_mv[w][:, h, :], gn_st[w][:, h, :]).then_inc(s_gag[w], 1)

            def group_deviation(w, e, b, k):
                i = await_filled(dve, b, k, f"gm{w}")
                v.tensor_copy(gn_mu[w][:, :], work[:, i, 0:CH]).then_inc(emptied[i], 1)
                await_emptied(dve, b, k, f"gm{w}")
                v.tensor_tensor(gn_dm[w][:, :], gn_mv[w][:, :, 0], gn_mu[w][:, :], ALU.subtract).then_inc(s_gdv[w], 1)
                dve.wait_ge(s_gdv[w], e * 3 + 1)
                v.tensor_tensor(gn_sq[w][:, :], gn_dm[w][:, :], gn_dm[w][:, :], ALU.mult).then_inc(s_gdv[w], 1)
                dve.wait_ge(s_gdv[w], e * 3 + 2)
                v.tensor_tensor(gn_dv[w][:, :], gn_sq[w][:, :], gn_mv[w][:, :, 1], ALU.add).then_inc(s_gdv[w], 1)

            def group_variance(w, b, k):
                i = await_filled(dve, b, k, f"gv{w}")
                v.tensor_scalar(gn_ve[w][:, :], work[:, i, 0:CH], GN_EPS, None, ALU.add).then_inc(emptied[i], 1)

            def charge(b, k, kc):
                cols = slice(kc * T, (kc + 1) * T)
                if kc == 0:
                    await_emptied(dve, b, 1, "b1")
                await_filled(dve, b, L1_AT[kc - 1] if kc > 0 else L1_AT[K - 1] - K, f"to{(kc - 1) % K}_1")
                for h in range(CH):
                    i = await_filled(dve, b, k, f"l{kc}_{h}")
                    v.scalar_tensor_tensor(out=ob[:, h, :], in0=work[:, i, 0:T], scalar=b1s[:, h:h + 1],
                                           in1=volt[:, h, cols], op0=ALU.add, op1=ALU.subtract).then_inc(emptied[i], 1)
                for h in range(CH):
                    await_emptied(dve, b, k, f"l{kc}_{h}")
                    v.scalar_tensor_tensor(out=volt[:, h, cols], in0=ob[:, h, :], scalar=0.5,
                                           in1=volt[:, h, cols], op0=ALU.mult, op1=ALU.add).then_inc(s_volt, 1)

            def fire(b, k, kc):
                il = (b - 1) * K + kc
                cols = slice(kc * T, (kc + 1) * T)
                for h in range(CH):
                    dve.wait_ge(s_volt, il * 4 + 1 + h)
                    v.scalar_tensor_tensor(out=ob[:, h, :], in0=volt[:, h, cols], scalar=1.0,
                                           in1=img[:, img_par(b, -1), h, cols], op0=ALU.is_ge,
                                           op1=ALU.add).then_inc(s_spike, 1)
                for h in range(CH):
                    v.scalar_tensor_tensor(out=volt[:, h, cols], in0=volt[:, h, cols], scalar=1.0,
                                           in1=volt[:, h, cols], op0=ALU.is_lt, op1=ALU.mult).then_inc(s_volt, 1)

            def accumulate(b, k, n, before):
                kq = (k - before) % K
                q = b * K + k - before
                i = q * NS + n
                for m in range(NT):
                    dve.wait_ge(s_ht, 3 * i + m + 1)
                    if n == 0:
                        if m == 0:
                            await_emptied(dve, b, k - 1, "ct")
                            hold("dve", dve, b)
                        await_emptied(dve, b, k - 1, f"yi{m}")
                    else:
                        dve.wait_ge(s_y, 3 * (i - 1) + m + 1)
                    j = (3 * n + m) % NHT
                    v.scalar_tensor_tensor(out=y[:, kq % 2, m, :], in0=ht[:, j, :],
                                           scalar=ct[:, kq % 2, m * NS + n:m * NS + n + 1],
                                           in1=y[:, kq % 2, m, :], op0=ALU.mult, op1=ALU.add).then_inc(s_y, 1)

            def iteration(b, k):
                do = does(b, k)
                q0, q1 = b * K + k - 1, b * K + k + 1
                k1 = (k + 1) % K
                p0, p1 = (k - 1) % 2, k1 % 2
                main, pre, post = "main" in do, PRE in do, POST in do
                for s in range(NS):
                    i = (b * K + k) * NS + s
                    j = (k * NS + s) % 3
                    if main:
                        dve.wait_ge(s_dec, i + 1)
                        dve.wait_ge(s_u, i + 1)
                        state = st[:, j, :, :].rearrange("p c t -> p (c t)")
                        v.tensor_tensor_scan(state, decay[:, s % 2, :, :].rearrange("p c t -> p (c t)"), state,
                                             0.0, ALU.mult, ALU.add).then_inc(s_scan, 1)
                    if s >= Y_LAG and main:
                        accumulate(b, k, s - Y_LAG, 0)
                    if s < Y_LAG and post:
                        accumulate(b, k, NS - Y_LAG + s, 1)
                    if s == 11 and pre:
                        dve.wait_ge(s_ln, q1 + 1)
                        v.scalar_tensor_tensor(out=dt[:, p1, :, :], in0=xb[:, :, :], scalar=0.0, in1=dt[:, p1, :, :],
                                               op0=ALU.max, op1=ALU.add).then_inc(s_dt, 1)
                    if s == Y_LAG - 1 and post:
                        for m in range(NT):
                            dve.wait_ge(s_y, (q0 * NS + NS - 1) * 3 + m + 1)
                            v.bn_stats(ln_st[:, m, :], y[:, p0, m, :]).then_inc(s_lnst, 1)
                        for m in range(NT):
                            dve.wait_ge(s_lnst, q0 * NT + m + 1)
                            hold("dve", dve, b)
                            v.bn_aggr(ln_mv[:, m, :], ln_st[:, m, :]).then_inc(s_lnmv, 1)
                        dve.wait_ge(s_lnmv, q0 * NT + NT)
                        v.tensor_scalar(ln_ve[:, :], ln_mv[:, :, 1], LN_EPS, None, ALU.add).then_inc(s_lnve, 1)
                    if L1 in do:
                        for kc, step, slot in lif_slots(k):
                            if slot == s and step == "charge":
                                charge(b, k, kc)
                    if s == 12 and pre:
                        need(dve, s_cast, q1 * 3)
                        jw = await_filled(dve, b, k, "dn")
                        v.scalar_tensor_tensor(out=bprod[:, :], in0=work[0:XP_ROWS, jw, 0:T], scalar=bn_rows[:, 0:1],
                                               in1=xp[:, :], op0=ALU.add, op1=ALU.mult).then_inc(emptied[jw], 1)
                    if s in (13, 14) and post:
                        h = s - 13
                        jw = await_filled(dve, b, k, f"wo{h}")
                        xs = img[:, img_par(b, -1 if k == 0 else 0), h, (k - 1) % K * T:((k - 1) % K + 1) * T]
                        v.scalar_tensor_tensor(out=xs, in0=work[:, jw, 0:T], scalar=bo[:, h:h + 1],
                                               in1=xs, op0=ALU.add, op1=ALU.add).then_inc(emptied[jw], 1)
                    if s in (14, 15) and post:
                        h, kc = s - 14, (k - 1) % K
                        await_emptied(dve, b, k, f"wo{h}")
                        hold("dve", dve, b)
                        v.bn_stats(gn_st[1][:, h, kc * 6:kc * 6 + 6],
                                   img[:, img_par(b, -1 if k == 0 else 0), h, kc * T:(kc + 1) * T]).then_inc(s_gst[1], 1)
                    if L1 in do:
                        for kc, step, slot in lif_slots(k):
                            if slot == s and step == "fire":
                                fire(b, k, kc)
                    if TIN in do and k in TIN_CHUNKS and s in (9, 11):
                        kc = TIN_CHUNKS[k][0 if s == 9 else 1]
                        for h in range(CH):
                            await_emptied(dve, b, k, f"ti{kc}_{h}")
                            hold("dve", dve, b)
                            v.bn_stats(gn_st[0][:, h, kc * 6:kc * 6 + 6],
                                       img[:, img_par(b, 1), h, kc * T:(kc + 1) * T]).then_inc(s_gst[0], 1)
                    if k == 4 and TIN in do:
                        if s == 11:
                            channel_means(0, b + 1)
                        if s == 12:
                            group_deviation(0, b + 1, b, k)
                        if s == 13:
                            group_variance(0, b, k)
                    if k == 1 and GN1 in do:
                        if s == 0:
                            channel_means(1, b - 1)
                        if s == 1:
                            group_deviation(1, b - 1, b, k)
                        if s == 2:
                            group_variance(1, b, k)
                    if k == 1 and s == 5 and GN1 in do:
                        jw = await_filled(dve, b, k, "b1")
                        v.tensor_tensor(b1s[:, :], work[:, jw, 0:CH], b1c[:, :], ALU.add).then_inc(emptied[jw], 1)

            walk(dve, iteration)

        @block.tensor
        def _(pe):
            t = nc.tensor
            pe.wait_ge(s_w1, 16)
            pe.wait_ge(s_set_pool, 2)
            for hi in range(CH):
                for ho in range(CH):
                    last = t.transpose(ht[:, 0, hi * C + ho * P:hi * C + (ho + 1) * P],
                                       w1s[:, ho, hi * P:(hi + 1) * P], ident[:, :])
            last.then_inc(s_setp, 1)
            pe.wait_ge(s_set_dve, 2)
            pe.wait_ge(s_set_pool, 4)

            def conv(b, k, c, lo, hi):
                i = turn(b, k, f"cv{c}")[0]
                if lo == 0:
                    pe.wait_ge(s_tri[c], (b * K + k + 2) * STEPS * 16)
                    claim(pe, b, k, f"cv{c}")
                for step in range(lo, hi):
                    g, dx = divmod(step, TAPS)
                    last = t.matmul(work[g * Q:(g + 1) * Q, i, 0:T].rearrange("p (r w) -> p r w", w=W),
                                    conv_w[:, c * NQ + g, dx, :], tri[:, c % 2, g, :, dx:dx + W],
                                    start=dx == 0, stop=dx == TAPS - 1)
                if hi == STEPS:
                    last.then_inc(filled[i], 1)

            def iteration(b, k):
                do = does(b, k)
                q0, q1 = b * K + k - 1, b * K + k + 1
                k1 = (k + 1) % K
                p0, p1 = (k - 1) % 2, k1 % 2
                main, pre = "main" in do, PRE in do
                xn0, xn1 = (k - 1) % 3, k1 % 3
                def transposes(n, before):
                    i = (b * K + k - before) * NS + n
                    j = ((k - before) * NS + n) % 3
                    pe.wait_ge(s_scan, i + 1)
                    for m in range(NT):
                        need(pe, s_y, NT * i + m - NHT + 1)
                        for c in range(DC):
                            last = t.transpose(ht[:, (NT * n + m) % NHT, c * P:(c + 1) * P],
                                               st[:, j, c, 1 + m * P:1 + (m + 1) * P], ident[:, :])
                        last.then_inc(s_ht, 1)

                for s in range(NS):
                    steps = groups(k, s)
                    behind = 1 if s < NS - 2 else 0
                    for kind, name in steps[:behind] + [("states", "")] + steps[behind:]:
                        if kind == "states":
                            if s > 0 and main:
                                transposes(s - 1, 0)
                            if s == 0 and POST in do:
                                transposes(NS - 1, 1)
                            continue
                        if kind not in do:
                            continue
                        bc, kc = following(b, k) if kind == PRE2 else (b, k)
                        i = claim(pe, bc, kc, name)
                        if name[:2] == "bb":
                            n = int(name[2:])
                            par = p1 if n < 2 else k % 2
                            if n < 2:
                                pe.wait_ge(s_cast, q1 * 3 + 3)
                            last = t.matmul(work[:, i, 0:T], one_hot[:, n:n + 1].to_broadcast([XP_ROWS, P]),
                                            bparts[:, par, :], start=True, stop=True)
                        elif name[:2] == "xh":
                            c = int(name[2:])
                            pe.wait_ge(s_xn, bc * K + kc + 2)
                            if c == 0 and kc == K - 1:
                                pe.wait_ge(s_edge, (bc + 1) * 2 + 1)
                            if c == 0 and kc == K - 2:
                                pe.wait_ge(s_edge, bc * 2 + 2)
                            for h in range(CH):
                                last = t.matmul(work[:, i, 0:HALO], win[:, h, c * P:(c + 1) * P],
                                                xn[:, (kc + 1) % 3, h, :], start=h == 0, stop=h == CH - 1)
                        elif name[0] == "z":
                            c = int(name[1:])
                            for h in range(CH):
                                last = t.matmul(work[:, i, 0:T], win[:, h, D + c * P:D + (c + 1) * P],
                                                xn[:, xn0, h, W:W + T], start=h == 0, stop=h == CH - 1)
                        elif name == "xp":
                            await_emptied(pe, b, k, f"cv{DC - 1}")
                            for c in range(DC):
                                last = t.matmul(work[0:XP_ROWS, i, 0:T], wxp[:, c, :], xc[:, p1, c, :],
                                                start=c == 0, stop=c == DC - 1)
                        elif name == "ct":
                            await_emptied(pe, b, k, "xp")
                            for m in range(NT):
                                last = t.transpose(work[:, i, m * XP_ROWS:(m + 1) * XP_ROWS], xp[:, m * P:(m + 1) * P],
                                                   ident[0:XP_ROWS, 0:XP_ROWS])
                        elif name[:2] == "dt":
                            c = int(name[2:])
                            await_emptied(pe, b, k, "xp")
                            last = t.matmul(work[:, i, 0:T], wdt[:, c * P:(c + 1) * P], xp[:, :], start=True, stop=True)
                        elif name == "dn":
                            pe.wait_ge(s_dt, q1 + 1)
                            for c in range(DC):
                                last = t.matmul(work[0:XP_ROWS, i, 0:T], wnp[:, c, :], dt[:, p1, c, :],
                                                start=c == 0, stop=c == DC - 1)
                        elif name[:2] == "bt":
                            pe.wait_ge(s_yn, q0 * NT + NT)
                            for o in range(4):
                                c, m = divmod(int(name[2:]) * 4 + o, NT)
                                last = t.transpose(work[:, i, o * P:(o + 1) * P], y[:, p0, m, c * P:(c + 1) * P],
                                                   ident[:, :])
                        elif name[:2] == "wo":
                            h = int(name[2:])
                            for c in range(DC):
                                pe.wait_ge(s_yz, q0 * DC + c + 1)
                                last = t.matmul(work[:, i, 0:T], wo[:, c, h * P:(h + 1) * P], zs[:, c, :],
                                                start=c == 0, stop=c == DC - 1)
                        elif name[:2] == "yi":
                            m = int(name[2:])
                            for c in range(DC):
                                last = t.matmul(work[:, i, c * P:(c + 1) * P], xc[:, p1, c, m * P:(m + 1) * P],
                                                skip_diag[:, c, :], start=True, stop=True)
                        elif name[:2] == "ti":
                            kc, h = int(name[2]), int(name[4])
                            pe.wait_ge(s_xin, ((b + 1) * K + kc + 1) * 16)
                            for m in range(NT):
                                last = t.transpose(work[:, i, m * P:(m + 1) * P], xin[:, m, h * P:(h + 1) * P],
                                                   ident[:, :])
                        elif name[0] == "l":
                            kc, h = int(name[1]), int(name[3])
                            pe.wait_ge(s_w1s, b)
                            for hi in range(CH):
                                last = t.matmul(work[:, i, 0:T], w1s[:, hi, h * P:(h + 1) * P],
                                                img[:, img_par(b, -1), hi, kc * T:(kc + 1) * T],
                                                start=hi == 0, stop=hi == CH - 1)
                        elif name[:2] == "to":
                            kc, half = int(name[2]), int(name[4])
                            pe.wait_ge(s_spike, ((b - 1) * K + kc) * CH + CH)
                            for m in ((0, 1) if half == 0 else (2,)):
                                for h in range(CH):
                                    o = (m - 2 * half) * C + h * P
                                    last = t.transpose(work[:, i, o:o + P], ob[:, h, m * P:(m + 1) * P],
                                                       ident[:, :])
                        elif name == "b1":
                            pe.wait_ge(s_gpl[1], (b - 1) * 3 + 3)
                            for ho in range(CH):
                                for hi in range(CH):
                                    last = t.matmul(work[:, i, ho:ho + 1], w1t[:, hi, ho * P:(ho + 1) * P],
                                                    gn_nb[1][:, hi:hi + 1], start=hi == 0, stop=hi == CH - 1)
                        elif name[:2] == "gm":
                            w = int(name[2])
                            e = b + 1 if w == 0 else b - 1
                            pe.wait_ge(s_gag[w], e * CH + CH)
                            last = t.matmul(work[:, i, 0:CH], group_mean[:, :], gn_mv[w][:, :, 0], start=True, stop=True)
                        elif name[:2] == "gv":
                            w = int(name[2])
                            e = b + 1 if w == 0 else b - 1
                            pe.wait_ge(s_gdv[w], e * 3 + 3)
                            last = t.matmul(work[:, i, 0:CH], group_mean[:, :], gn_dv[w][:, :], start=True, stop=True)
                        last.then_inc(filled[i], 1)
                    for part in CONV_PARTS.get(s, ()):
                        if pre:
                            conv(b, k, *part)

            walk(pe, iteration)


_INS = ['x', 'L0_conv_W_in', 'L0_conv_conv_k', 'L0_conv_W_xproj', 'L0_conv_W_dt', 'L0_conv_b_dt', 'L0_conv_A_log',
        'L0_conv_Dskip', 'L0_conv_W_dtN', 'L0_conv_b_dtN', 'L0_conv_ln_g', 'L0_conv_ln_b', 'L0_conv_W_out',
        'L0_conv_b_out', 'L1_conv_W', 'L1_conv_b']
_OUTS = [((B, H, W, C), 'float32')]


def kernel(**inputs):
    import numpy as _np
    import concourse.bacc as _bacc
    from concourse import mybir as _mybir
    from concourse.bass_utils import run_bass_kernel_spmd as _run

    nc = _bacc.Bacc("TRN2", target_bir_lowering=False, num_devices=1)
    arrays, args = {}, []
    for name in _INS:
        a = _np.ascontiguousarray(inputs[name])
        arrays[f"in_{name}_dram"] = a
        args.append(nc.dram_tensor(f"in_{name}_dram", a.shape, _mybir.dt.from_np(a.dtype), kind="ExternalInput").ap())
    for i, (shape, dtype) in enumerate(_OUTS):
        dt = _mybir.dt.from_np(_np.dtype(dtype))
        args.append(nc.dram_tensor(f"out_{i}_dram", shape, dt, kind="ExternalOutput").ap())
    vssm_lif_kernel(nc, *args)
    r = _run(nc, [arrays], core_ids=[0])
    got = tuple(r.results[0][f"out_{i}_dram"] for i in range(len(_OUTS)))
    return got[0]
```
